# Optimizing a Trainium2 kernel written in Bass

```python
import numpy as np
import jax
import jax.numpy as jnp

def _softmax(x, axis=-1):
    return jax.nn.softmax(x, axis=axis)

def _gelu(x):
    return jax.nn.gelu(x, approximate=True)

def _silu(x):
    return jax.nn.silu(x)

def _sigmoid(x):
    return jax.nn.sigmoid(x)

def _layernorm(x, axis=-1, eps=1e-05):
    m = jnp.mean(x, axis=axis, keepdims=True)
    v = jnp.var(x, axis=axis, keepdims=True)
    return (x - m) / jnp.sqrt(v + eps)

def _scatter_add(tgt, idx, src, axis=0):
    return tgt.at[idx].add(src)

def _segment_sum(src, seg, n):
    return jax.ops.segment_sum(src, seg, n)
kernel_name = 'mk_conv_preact_d1_conv_nchw512_r4_39bca0'

def setup_inputs(seed: int=0):
    np.random.seed(seed)
    _w = jnp.asarray

    def _rec_inputs():
        import jax
        import jax.numpy as jnp
        _gk = jax.random.key(seed)
        x = -0.000125 + 0.9999 * jax.random.normal(jax.random.fold_in(_gk, 1), (4, 128, 32, 32), jnp.float32)
        return x
    x = _rec_inputs()

    def _L0_conv_setup():
        import jax, jax.numpy as jnp
        import numpy as np
        WS = 2
        NH = 8

        def window_attn(x, Wqkv, bqkv, scale, ws=WS, nh=NH):
            B, H, W, C = x.shape
            hg, wg = (H // ws, W // ws)
            hd = C // nh
            xw = x.reshape(B, hg, ws, wg, ws, C).transpose(0, 1, 3, 2, 4, 5)
            qkv = (xw @ Wqkv + bqkv).reshape(B, hg * wg, ws * ws, 3, nh, hd)
            q, k, v = jnp.transpose(qkv, (3, 0, 1, 4, 2, 5))
            attn = jax.nn.softmax(jnp.einsum('bgnqd,bgnkd->bgnqk', q, k) * scale, axis=-1)
            o = jnp.einsum('bgnqk,bgnkd->bgnqd', attn, v)
            o = o.transpose(0, 1, 3, 2, 4).reshape(B, hg, wg, ws, ws, C)
            return o.transpose(0, 1, 3, 2, 4, 5).reshape(B, H, W, C)
        key = jax.random.key(seed)
        k1, k2, k3, k4, k5 = jax.random.split(key, 5)
        B, C, H, W = (4, 128, 32, 32)
        x = jax.random.normal(k1, (B, C, H, W), dtype=jnp.float32)
        Wqkv = jax.random.normal(k2, (C, 3 * C), dtype=jnp.float32) * 0.02
        bqkv = jax.random.normal(k3, (3 * C,), dtype=jnp.float32) * 0.02
        Wproj = jax.random.normal(k4, (C, C), dtype=jnp.float32) * 0.02
        bproj = jax.random.normal(k5, (C,), dtype=jnp.float32) * 0.02
        return {'x': x, 'Wqkv': Wqkv, 'bqkv': bqkv, 'Wproj': Wproj, 'bproj': bproj}
    _L0_conv_all = _L0_conv_setup()
    _L0_conv_in = {k: v for k, v in _L0_conv_all.items() if k in ('Wqkv', 'bqkv', 'Wproj', 'bproj')}
    del _L0_conv_all
    return {'x': x, 'L0_conv_Wqkv': _L0_conv_in['Wqkv'], 'L0_conv_bqkv': _L0_conv_in['bqkv'], 'L0_conv_Wproj': _L0_conv_in['Wproj'], 'L0_conv_bproj': _L0_conv_in['bproj']}

def reference(x, L0_conv_Wqkv, L0_conv_bqkv, L0_conv_Wproj, L0_conv_bproj):
    import jax
    import jax.numpy as jnp

    def _L0_conv_ref(x, Wqkv, bqkv, Wproj, bproj):
        import jax, jax.numpy as jnp
        import numpy as np
        WS = 2
        NH = 8

        def window_attn(x, Wqkv, bqkv, scale, ws=WS, nh=NH):
            B, H, W, C = x.shape
            hg, wg = (H // ws, W // ws)
            hd = C // nh
            xw = x.reshape(B, hg, ws, wg, ws, C).transpose(0, 1, 3, 2, 4, 5)
            qkv = (xw @ Wqkv + bqkv).reshape(B, hg * wg, ws * ws, 3, nh, hd)
            q, k, v = jnp.transpose(qkv, (3, 0, 1, 4, 2, 5))
            attn = jax.nn.softmax(jnp.einsum('bgnqd,bgnkd->bgnqk', q, k) * scale, axis=-1)
            o = jnp.einsum('bgnqk,bgnkd->bgnqd', attn, v)
            o = o.transpose(0, 1, 3, 2, 4).reshape(B, hg, wg, ws, ws, C)
            return o.transpose(0, 1, 3, 2, 4, 5).reshape(B, H, W, C)
        B, C, H, W = x.shape
        scale = (C // NH) ** (-0.5)
        xr = x.reshape(B, H, W, C)
        g = window_attn(xr, Wqkv, bqkv, scale) @ Wproj + bproj
        l = xr.reshape(B, C, H, W)
        l = l.reshape(B, C, H // 2, 2, W // 2, 2).mean(axis=(3, 5))
        h, w = (H // 2, W // 2)
        l = l.reshape(B, h, w, C)
        l = window_attn(l, Wqkv, bqkv, scale)
        l = l.reshape(B, C, h, w)
        px = jnp.pad(l, ((0, 0), (0, 0), (1, 0), (0, 0)), mode='reflect')
        lx = 0.5 * (px[:, :, :-1, :] + px[:, :, 1:, :])
        py = jnp.pad(l, ((0, 0), (0, 0), (0, 0), (0, 1)), mode='reflect')
        ly = 0.5 * (py[..., :-1] + py[..., 1:])
        l = jax.image.resize(lx + ly, (B, C, H, W), method='bilinear')
        l = l.reshape(B, H, W, C)
        return (g + l).transpose(0, 3, 1, 2)

    def _gn(v, G=32, eps=1e-05):
        B_, C_, H_, W_ = v.shape
        g = v.reshape(B_, G, C_ // G, H_, W_)
        m = jnp.mean(g, axis=(2, 3, 4), keepdims=True)
        s = jnp.var(g, axis=(2, 3, 4), keepdims=True)
        return ((g - m) / jnp.sqrt(s + eps)).reshape(v.shape)

    def _ln_c(v, eps=1e-06):
        m = jnp.mean(v, axis=1, keepdims=True)
        s = jnp.var(v, axis=1, keepdims=True)
        return (v - m) / jnp.sqrt(s + eps)

    def _ln_t(v, eps=1e-05):
        m = jnp.mean(v, axis=-1, keepdims=True)
        s = jnp.var(v, axis=-1, keepdims=True)
        return (v - m) / jnp.sqrt(s + eps)

    def _to_tokens(v):
        B_, C_, H_, W_ = v.shape
        return v.reshape(B_, C_, H_ * W_).transpose(0, 2, 1)

    def _from_tokens(t, like):
        B_, C_, H_, W_ = like.shape
        return t.transpose(0, 2, 1).reshape(B_, C_, H_, W_)
    x = x + _L0_conv_ref(_gn(x), L0_conv_Wqkv, L0_conv_bqkv, L0_conv_Wproj, L0_conv_bproj)
    return x

_drawn_inputs = setup_inputs


def setup_inputs(seed=0):
    import zlib

    import numpy as np

    out = dict(_drawn_inputs(seed))
    spreads = {}
    factors = {'L0_conv_bproj': 2.777}
    for name, (base, spread) in spreads.items():
        noise = np.random.default_rng([zlib.crc32(name.encode()), seed]).standard_normal(out[name].shape)
        drawn = base * np.exp(spread * noise) if base else spread * noise
        out[name] = jnp.asarray(drawn.astype(out[name].dtype))
    for name, factor in factors.items():
        out[name] = (out[name] * factor).astype(out[name].dtype)
    return out
```

```python
from contextlib import ExitStack

import numpy as np

import concourse.bass as bass
from concourse import mybir

ALU = mybir.AluOpType
ACT = mybir.ActivationFunctionType
AX = mybir.AxisListType
F32 = mybir.dt.float32
BF16 = mybir.dt.bfloat16

B, C, H, W = 4, 128, 32, 32
PIX = H * W
P = 128
K = PIX // P
HEADS = 8
HD = C // HEADS
GROUP = 4
EPS = 1e-5
WIN = 4
TILE_W = 128
PAIRS = WIN * WIN
NS = PAIRS * HEADS
SCALE = HD ** -0.5
DVE_QUERIES = 3
POOL_QUERIES = WIN - DVE_QUERIES
HALVES = 2
CH = C // HALVES
TOK = CH * K
PH, PW = H // 2, W // 2
KL = PH * PW // P

TILES = [(0, 0), (0, 1), (None, 0), (1, 0), (1, 1), (None, 1), (2, 0), (2, 1), (3, 0), (3, 1)]
N = len(TILES)
POOLED = [n for n, t in enumerate(TILES) if t[0] is None]
FULL = [n for n, t in enumerate(TILES) if t[0] is not None]

STATS = [(0, 1), (1, 3)]

STEPS = range(-1, N + 1)
EARLY = {-1: [("mean", 1), ("var", 1)], 0: [("xt", 1, 0), ("xt", 1, 1), ("lt", 0)], 2: [("xt", 2, 0)], 3: [("xt", 2, 1)], 4: [("xt", 3, 0)],
         5: [("xt", 3, 1)]}
LATE = {2: [("lt", 1)], 3: [("out", 0)], 4: [("out", 1)], 5: [("out", 3)],
        6: [("out", 4)], 7: [("out", 6)], 8: [("out", 7)], 9: [("out", 8)], 10: [("out", 9)]}
PROLOGUE = [("mean", 0), ("var", 0), ("xt", 0, 0), ("xt", 0, 1)]
JOBS = PROLOGUE + [j for s in STEPS for j in EARLY.get(s, []) + LATE.get(s, [])]


def jobs_of(kinds):
    return [j for j in JOBS if j[0] in kinds]


def resize_blocks():
    def blur(n, front):
        m = np.zeros((n, n))
        for i in range(n):
            other = (i - 1 if i else 1) if front else (i + 1 if i < n - 1 else n - 2)
            m[i, i] += 0.5
            m[i, other] += 0.5
        return m

    def double(n):
        m = np.zeros((2 * n, n))
        for i in range(n):
            m[2 * i, i] += 0.75
            m[2 * i, max(i - 1, 0)] += 0.25
            m[2 * i + 1, i] += 0.75
            m[2 * i + 1, min(i + 1, n - 1)] += 0.25
        return m

    up_y, up_x = double(PH), double(PW)
    r = np.kron(up_y @ blur(PH, True), up_x) + np.kron(up_y, up_x @ blur(PW, False))
    r = r.T.reshape(KL, P, K, P)
    used = [(k, l) for k in range(K) for l in range(KL) if r[l, :, k].any()]
    return used, np.stack([r[l, :, k] for k, l in used], 1).astype(np.float32)


BLOCKS, RESIZE = resize_blocks()


def conv_attention_kernel(nc, x, w_qkv, b_qkv, w_proj, b_proj, resize, out):
    x_dram = x.rearrange("b c h w -> b c (h w)")
    out_dram = out.rearrange("b f h w -> b f (h w)")

    with ExitStack() as ctx:
        def sb(name, shape, dt=F32):
            return ctx.enter_context(nc.sbuf_tensor(name, shape, dt))

        def psum(name):
            return ctx.enter_context(nc.psum_tensor(name, [P, 512], F32))

        def sem(name):
            return ctx.enter_context(nc.semaphore(name))

        ident = sb("ident", [P, P])
        group_mean = sb("group_mean", [P, P])
        ones3 = sb("ones3", [3, P], BF16)
        half_pow = sb("half_pow", [P, B])
        w_sb = sb("w_sb", [P, 3 * C])
        wqk = sb("wqk", [P, 2, C])
        wp_sb = sb("wp_sb", [P, C])
        resize_sb = sb("resize_sb", [P, len(BLOCKS), P])
        bias3 = sb("bias3", [3, 2 * C])
        part = sb("part", [3, 3, 2 * C], BF16)
        rest = sb("rest", [3, 2, 2 * C])
        picked = sb("picked", [3, 2, 2 * C], BF16)
        bias_qk = sb("bias_qk", [3, 2 * C], BF16)
        bias_v = sb("bias_v", [P, 1])
        bias_p = sb("bias_p", [P, 1])
        x_sb = sb("x_sb", [P, B, PIX])
        xn = sb("xn", [P, B, PIX])
        rows2 = sb("rows2", [P, B, H * PW])
        pooled = sb("pooled", [P, B, PH * PW])
        bn = sb("bn", [P, B, 2, 6])
        mv = sb("mv", [P, B, 2])
        gstat = sb("gstat", [P, B, 2])
        dev = sb("dev", [P, B])
        dev2 = sb("dev2", [P, B])
        gvar = sb("gvar", [P, B])
        rstd = sb("rstd", [P, B])
        xt = sb("xt", [P, B, K * C])
        lt = sb("lt", [P, 2, 2 * KL * C])
        ot = sb("ot", [P, N, 512])
        out_sb = sb("out_sb", [P, N, TOK])
        q_sb = sb("q_sb", [P, 2, POOL_QUERIES * C])
        k_sb = sb("k_sb", [P, 2, WIN * C])
        v_sb = sb("v_sb", [P, 2, WIN * C])
        qk = sb("qk", [P, 2, PAIRS * C])
        pv = sb("pv", [P, 2, PAIRS * C])
        st_sb = sb("st_sb", [P, 2, TILE_W])
        row_max = sb("row_max", [P, 2, WIN * HEADS])
        shifted = sb("shifted", [P, 2, NS])
        expd = sb("expd", [P, 2, NS])
        denom = sb("denom", [P, 2, WIN * HEADS])
        inv = sb("inv", [P, 2, WIN * HEADS])
        prob = sb("prob", [P, 2, POOL_QUERIES * WIN * HEADS])

        q_ps = [psum("q_ps0"), psum("q_ps1")]
        k_ps = psum("k_ps")
        v_ps = psum("v_ps")
        sm_ps = [psum("sm_ps0"), psum("sm_ps1")]
        ot_ps = psum("ot_ps")
        job_ps = psum("job_ps")
        ST, SC, PR = slice(0, TILE_W), slice(TILE_W, TILE_W + NS), slice(2 * NS, 2 * NS + DVE_QUERIES * WIN * HEADS)

        x_loaded = [sem(f"x_loaded{b}") for b in range(B)]
        w_loaded, bias_loaded, bv_loaded, bp_loaded, wp_loaded, resize_loaded = (
            sem("w_loaded"), sem("bias_loaded"), sem("bv_loaded"), sem("bp_loaded"), sem("wp_loaded"),
            sem("resize_loaded"))
        out_stored = sem("out_stored")
        consts_set, consts_made = sem("consts_set"), sem("consts_made")
        bias_step, bias_made = sem("bias_step"), sem("bias_made")
        wqk_made = sem("wqk_made")
        bn_done, mv_done, gmean_read, dev_done, dev2_done, gvar_done = (
            sem("bn_done"), sem("mv_done"), sem("gmean_read"), sem("dev_done"), sem("dev2_done"), sem("gvar_done"))
        rstd_done, xn_done, rows_done, pooled_done = sem("rstd_done"), sem("xn_done"), sem("rows_done"), sem("pooled_done")
        qk_made, kq_out, v_made, v_out = sem("qk_made"), sem("kq_out"), sem("v_made"), sem("v_out")
        qk_dve, qk_pool, st_made, st_out, s_made = (
            sem("qk_dve"), sem("qk_pool"), sem("st_made"), sem("st_out"), sem("s_made"))
        max_done, shift_done, exp_done, denom_done, inv_done, prob_done = (
            sem("max_done"), sem("shift_done"), sem("exp_done"), sem("denom_done"), sem("inv_done"), sem("prob_done"))
        pv_dve, pv_pool, ot_made, ot_out = sem("pv_dve"), sem("pv_pool"), sem("ot_made"), sem("ot_out")
        job_made, job_act, job_dve = sem("job_made"), sem("job_act"), sem("job_dve")

        ACT_JOBS = jobs_of(("xt", "lt"))
        DVE_JOBS = jobs_of(("mean", "var", "out"))

        def after_reader(eng, job):
            if job in ACT_JOBS:
                eng.wait_ge(job_act, ACT_JOBS.index(job) + 1)
            else:
                eng.wait_ge(job_dve, DVE_JOBS.index(job) + 1)

        xt_view = xt[:, :, :].rearrange("f b (r s T w) -> f b r s T w", r=2, s=2, T=2)
        xt_rows = xt[:, :, :].rearrange("f b (n g m) -> f b g n m", g=2, m=8)
        job_full = job_ps[:, :].rearrange("f (r s n k2 c4) -> f k2 s n r c4", r=2, s=2, n=16, k2=2)
        ot_full = ot_ps[:, :].rearrange("f (k2 s i r c4) -> f s r i k2 c4", k2=4, s=2, i=8, r=2)
        ident_full = ident[:, :].rearrange("p (a b c) -> p a b c", a=8, b=4)
        ident_chan = ident[:, :].rearrange("p (a b c) -> p a b c", a=16, b=2)
        lt_view = lt[:, :, :].rearrange("f g (r s w) -> f g r s w", r=2, s=2)
        job_pool = job_ps[:, :].rearrange("f (r s b i j) -> f b s i r j", r=2, s=2, b=2, i=8)
        ot_pool = ot_ps[:, :].rearrange("f (b s i r j) -> f s r b i j", b=2, s=2, i=8, r=2)
        ident_pool = ident[:, :].rearrange("p (a b c) -> p a b c", a=2, b=8)
        ident_pchan = ident[:, :].rearrange("p (a b c) -> p a b c", a=8, b=2)

        def tokens(n, r, s):
            b, half = TILES[n]
            return lt_view[:, half, r, s] if b is None else xt_view[:, b, r, s, half]

        def query_key_operands(n, query, queries, i):
            to = qk[:, n % 2, :].rearrange("w (d q k h) -> w q k d h", d=HD, q=WIN, k=WIN)[:, query]
            q = queries[:, i * C:(i + 1) * C].rearrange("w (d h) -> w d h", d=HD).unsqueeze(1)
            keys = k_sb[:, n % 2, :].rearrange("w (k d h) -> w k d h", k=WIN, d=HD)
            return to, q.broadcast_to([P, WIN, HD, HEADS]), keys

        block = ctx.enter_context(nc.Block())

        @block.sync
        def _(sp):
            for b in range(B):
                sp.dma_start(x_sb[:, b, :], x_dram[b]).then_inc(x_loaded[b], 16)
            for i, (_, n) in enumerate(jobs_of(("out",))):
                b, half = TILES[n]
                sp.wait_ge(job_dve, DVE_JOBS.index(("out", n)) + 1)
                sp.dma_start(out_dram[b, :, half * TOK:(half + 1) * TOK], out_sb[:, n, :]).then_inc(out_stored, 16)
            sp.wait_ge(out_stored, 16 * len(FULL))

        @block.gpsimd
        def _(pool):
            nc.gpsimd.memset(ident[:, :], 0.0).then_inc(consts_set, 1)
            nc.gpsimd.memset(group_mean[:, :], 1.0 / GROUP).then_inc(consts_set, 1)
            nc.gpsimd.memset(half_pow[:, :], -0.5).then_inc(consts_set, 1)
            nc.gpsimd.memset(ones3[:, :], 1.0).then_inc(consts_set, 1)
            pool.wait_ge(consts_set, 4)
            nc.gpsimd.affine_select(out=ident[:, :], in_=ident[:, :], compare_op=ALU.not_equal, fill=1.0, base=0,
                                    pattern=[[-1, P]], channel_multiplier=1).then_inc(consts_made, 1)
            gm = group_mean[:, :].rearrange("p (g c) -> p g c", c=GROUP)
            nc.gpsimd.affine_select(out=gm, in_=gm, compare_op=ALU.is_ge, fill=0.0, base=0,
                                    pattern=[[-GROUP, P // GROUP], [0, GROUP]],
                                    channel_multiplier=1).then_inc(consts_set, 1)
            pool.wait_ge(consts_set, 5)
            nc.gpsimd.affine_select(out=gm, in_=gm, compare_op=ALU.is_ge, fill=0.0, base=GROUP - 1,
                                    pattern=[[GROUP, P // GROUP], [0, GROUP]],
                                    channel_multiplier=-1).then_inc(consts_made, 1)
            pool.wait_ge(bias_loaded, 16 * 3)
            pool.wait_ge(consts_made, 2)
            src = bias3[:, :].rearrange("p (a h d) -> p a d h", a=2, h=HEADS)
            steps = 0

            def step(ins):
                nonlocal steps
                steps += 1
                ins.then_inc(bias_step, 1)
                pool.wait_ge(bias_step, steps)

            first = part[:, 0, :].rearrange("p (a d h) -> p a d h", a=2, d=HD)
            r0 = rest[:, 0, :].rearrange("p (a d h) -> p a d h", a=2, d=HD)
            for a in range(2):
                step(nc.gpsimd.tensor_copy(first[:, a], src[:, a]))
                step(nc.gpsimd.tensor_tensor(r0[:, a], src[:, a], first[:, a], ALU.subtract))
            step(nc.gpsimd.tensor_copy(part[:, 1, :], rest[:, 0, :]))
            step(nc.gpsimd.tensor_tensor(rest[:, 1, :], rest[:, 0, :], part[:, 1, :], ALU.subtract))
            step(nc.gpsimd.tensor_copy(part[:, 2, :], rest[:, 1, :]))
            step(nc.gpsimd.tensor_scalar(picked[:, 0, :], part[:, 0, :], ident[0:3, 0:1], None, ALU.mult))
            step(nc.gpsimd.tensor_scalar(picked[:, 1, :], part[:, 1, :], ident[0:3, 1:2], None, ALU.mult))
            step(nc.gpsimd.tensor_tensor(picked[:, 0, :], picked[:, 0, :], picked[:, 1, :], ALU.add))
            step(nc.gpsimd.tensor_scalar(picked[:, 1, :], part[:, 2, :], ident[0:3, 2:3], None, ALU.mult))
            nc.gpsimd.tensor_tensor(bias_qk[:, :], picked[:, 0, :], picked[:, 1, :], ALU.add).then_inc(bias_made, 1)

            def inverse_std(g):
                b0, nb = STATS[g]
                pool.wait_ge(gvar_done, g + 1)
                nc.gpsimd.tensor_tensor(rstd[:, b0:b0 + nb], gvar[:, b0:b0 + nb], half_pow[:, b0:b0 + nb],
                                        ALU.pow).then_inc(rstd_done, 1)

            def average_pool(b):
                pool.wait_ge(xn_done, b + 1)
                pix = xn[:, b, :].rearrange("c (y x s) -> c s y x", s=2, x=PW)
                nc.gpsimd.tensor_tensor(rows2[:, b, :].rearrange("c (y x) -> c y x", x=PW), pix[:, 0], pix[:, 1],
                                        ALU.add).then_inc(rows_done, 1)
                pool.wait_ge(rows_done, b + 1)
                row = rows2[:, b, :].rearrange("c (y s x) -> c s y x", s=2, x=PW)
                nc.gpsimd.tensor_tensor(pooled[:, b, :].rearrange("c (y x) -> c y x", x=PW), row[:, 0], row[:, 1],
                                        ALU.add).then_inc(pooled_done, 1)

            def query_key(n):
                pool.wait_ge(kq_out, 2 * (n + 1))
                if n >= 2:
                    pool.wait_ge(st_made, n - 1)
                for i in range(POOL_QUERIES):
                    ins = nc.gpsimd.tensor_tensor(*query_key_operands(n, DVE_QUERIES + i, q_sb[:, n % 2, :], i),
                                                  ALU.mult)
                ins.then_inc(qk_pool, 1)

            def prob_value(n):
                pool.wait_ge(prob_done, 2 * (n + 1))
                pool.wait_ge(v_out, n + 1)
                if n >= 2:
                    pool.wait_ge(ot_made, n - 1)
                o = pv[:, n % 2, :].rearrange("w (q kh d) -> w q kh d", q=WIN, d=HD)[:, DVE_QUERIES:]
                p = prob[:, n % 2, :].rearrange("w (q kh) -> w q kh", q=POOL_QUERIES)
                v = v_sb[:, n % 2, :].rearrange("w (kh d) -> w kh d", d=HD)
                for i in range(POOL_QUERIES):
                    ins = nc.gpsimd.tensor_tensor(o[:, i], p[:, i].unsqueeze(2).broadcast_to([P, WIN * HEADS, HD]), v,
                                                  ALU.mult)
                ins.then_inc(pv_pool, 1)

            inverse_std(0)
            inverse_std(1)
            query_key(0)
            average_pool(0)
            average_pool(1)
            for n in range(N):
                if n + 1 < N:
                    query_key(n + 1)
                if n < 2:
                    average_pool(n + 2)
                prob_value(n)

        @block.scalar
        def _(act):
            act.dma_start(w_sb[:, :], w_qkv).then_inc(w_loaded, 16)
            for i in range(3):
                act.dma_start(bias3[i:i + 1, :], b_qkv[0:2 * C].rearrange("(a n) -> a n", a=1)).then_inc(bias_loaded, 16)
            act.dma_start(bias_v[:, :], b_qkv[2 * C:3 * C].rearrange("(p a) -> p a", a=1)).then_inc(bv_loaded, 16)
            act.dma_start(bias_p[:, :], b_proj.rearrange("(p a) -> p a", a=1)).then_inc(bp_loaded, 16)
            act.dma_start(wp_sb[:, :], w_proj).then_inc(wp_loaded, 16)
            act.dma_start(resize_sb[:, :, :], resize).then_inc(resize_loaded, 16)
            act.wait_ge(w_loaded, 16)
            for a in range(2):
                nc.scalar.copy(wqk[:, a, :].rearrange("c (d h) -> c d h", d=HD),
                               w_sb[:, a * C:(a + 1) * C].rearrange("c (h d) -> c d h", h=HEADS)).then_inc(wqk_made, 1)

            def read_job(job):
                act.wait_ge(job_made, JOBS.index(job) + 1)
                if job[0] == "xt":
                    _, b, half = job
                    nc.scalar.copy(xt_rows[:, b, half], job_ps[:, :].rearrange("f (n m) -> f n m", m=8)
                                   ).then_inc(job_act, 1)
                else:
                    nc.scalar.mul(lt[:, job[1], :], job_ps[:, :], 0.25).then_inc(job_act, 1)

            def queries_keys_out(n):
                act.wait_ge(qk_made, n + 1)
                if n >= 2:
                    act.wait_ge(qk_dve, n - 1)
                    act.wait_ge(qk_pool, n - 1)
                nc.scalar.copy(q_sb[:, n % 2, :], q_ps[n % 2][:, DVE_QUERIES * C:]).then_inc(kq_out, 1)
                nc.scalar.copy(k_sb[:, n % 2, :], k_ps[:, :]).then_inc(kq_out, 1)

            def values_out(n):
                act.wait_ge(v_made, n + 1)
                if n >= 2:
                    act.wait_ge(pv_dve, n - 1)
                    act.wait_ge(pv_pool, n - 1)
                nc.scalar.copy(v_sb[:, n % 2, :], v_ps[:, :]).then_inc(v_out, 1)

            def scores_t_out(n):
                act.wait_ge(st_made, n + 1)
                if n >= 2:
                    act.wait_ge(s_made, n - 1)
                nc.scalar.copy(st_sb[:, n % 2, :], sm_ps[n % 2][:, ST]).then_inc(st_out, 1)

            def exponent(n):
                act.wait_ge(shift_done, n + 1)
                if n >= 2:
                    act.wait_ge(prob_done, 2 * (n - 1))
                nc.scalar.activation(expd[:, n % 2, :], shifted[:, n % 2, :], ACT.Exp, scale=SCALE).then_inc(exp_done, 1)

            def attention_out(n):
                act.wait_ge(ot_made, n + 1)
                nc.scalar.activation(ot[:, n, :], ot_ps[:, :], ACT.Identity, bias=bias_v[:, 0:1]).then_inc(ot_out, 1)

            for job in PROLOGUE:
                if job in ACT_JOBS:
                    read_job(job)
            act.wait_ge(bv_loaded, 16)
            for s in [-2] + list(STEPS):
                if 0 <= s < N:
                    exponent(s)
                if 0 <= s - 1:
                    attention_out(s - 1)
                for job in EARLY.get(s, []):
                    if job in ACT_JOBS:
                        read_job(job)
                if s + 2 < N:
                    queries_keys_out(s + 2)
                if 0 <= s + 1 < N:
                    scores_t_out(s + 1)
                if s + 2 < N:
                    values_out(s + 2)
                for job in LATE.get(s, []):
                    if job in ACT_JOBS:
                        read_job(job)

        @block.vector
        def _(dve):
            def batch_stats(g):
                b0, nb = STATS[g]
                for b in range(b0, b0 + nb):
                    dve.wait_ge(x_loaded[b], 16)
                    for i in range(2):
                        nc.vector.bn_stats(bn[:, b, i, :], x_sb[:, b, i * 512:(i + 1) * 512]).then_inc(bn_done, 1)
                for b in range(b0, b0 + nb):
                    dve.wait_ge(bn_done, 2 * (b + 1))
                    nc.vector.bn_aggr(mv[:, b, :], bn[:, b, :, :].rearrange("p i s -> p (i s)")).then_inc(mv_done, 1)

            def spread(g):
                b0, nb = STATS[g]
                bs = slice(b0, b0 + nb)
                dve.wait_ge(job_made, JOBS.index(("mean", g)) + 1)
                dve.wait_ge(mv_done, b0 + nb)
                nc.vector.tensor_copy(gstat[:, bs, :], job_ps[:, 0:2 * nb].rearrange("p (b s) -> p b s", s=2)
                                      ).then_inc(job_dve, 1)
                dve.wait_ge(job_dve, DVE_JOBS.index(("mean", g)) + 1)
                nc.vector.tensor_tensor(dev[:, bs], mv[:, bs, 0], gstat[:, bs, 0], ALU.subtract).then_inc(dev_done, 1)
                dve.wait_ge(dev_done, g + 1)
                nc.vector.tensor_tensor(dev2[:, bs], dev[:, bs], dev[:, bs], ALU.mult).then_inc(dev2_done, 1)

            def variance(g):
                b0, nb = STATS[g]
                bs = slice(b0, b0 + nb)
                dve.wait_ge(job_made, JOBS.index(("var", g)) + 1)
                nc.vector.scalar_tensor_tensor(out=gvar[:, bs], in0=job_ps[:, 0:nb], scalar=EPS, in1=gstat[:, bs, 1],
                                               op0=ALU.add, op1=ALU.add).then_inc(job_dve, 1)
                dve.wait_ge(job_dve, DVE_JOBS.index(("var", g)) + 1)
                nc.vector.tensor_copy(dev[:, bs], gvar[:, bs]).then_inc(gvar_done, 1)

            def normalise(g):
                b0, nb = STATS[g]
                dve.wait_ge(rstd_done, g + 1)
                for b in range(b0, b0 + nb):
                    nc.vector.tensor_scalar(xn[:, b, :], x_sb[:, b, :], gstat[:, b, 0:1], rstd[:, b:b + 1],
                                            ALU.subtract, ALU.mult).then_inc(xn_done, 1)

            def query_key(n):
                dve.wait_ge(kq_out, 2 * (n + 1))
                if n >= 2:
                    dve.wait_ge(st_made, n - 1)
                for i in range(DVE_QUERIES):
                    ins = nc.vector.tensor_tensor(*query_key_operands(n, i, q_ps[n % 2][:, :], i), ALU.mult)
                ins.then_inc(qk_dve, 1)

            def by_key(ap):
                return ap.rearrange("w (q k h) -> w q k h", q=WIN, k=WIN)

            def by_head(ap):
                return ap.rearrange("w (q h) -> w q h", q=WIN)

            def shift(n):
                dve.wait_ge(s_made, n + 1)
                sc = sm_ps[n % 2][:, SC]
                nc.vector.tensor_reduce(by_head(row_max[:, n % 2, :]),
                                        sc.rearrange("w (q k h) -> w q h k", q=WIN, k=WIN), AX.X,
                                        ALU.max).then_inc(max_done, 1)
                dve.wait_ge(max_done, n + 1)
                if n >= 2:
                    dve.wait_ge(exp_done, n - 1)
                nc.vector.tensor_tensor(by_key(shifted[:, n % 2, :]), by_key(sc),
                                        by_head(row_max[:, n % 2, :]).unsqueeze(2).broadcast_to([P, WIN, WIN, HEADS]),
                                        ALU.subtract).then_inc(shift_done, 1)

            def divide(n):
                dve.wait_ge(exp_done, n + 1)
                e = expd[:, n % 2, :]
                nc.vector.tensor_reduce(by_head(denom[:, n % 2, :]),
                                        e.rearrange("w (q k h) -> w q h k", q=WIN, k=WIN), AX.X,
                                        ALU.add).then_inc(denom_done, 1)
                dve.wait_ge(denom_done, n + 1)
                nc.vector.reciprocal(inv[:, n % 2, :], denom[:, n % 2, :]).then_inc(inv_done, 1)
                dve.wait_ge(inv_done, n + 1)
                if n >= 2:
                    dve.wait_ge(pv_pool, n - 1)
                by_q = by_head(inv[:, n % 2, :]).unsqueeze(2).broadcast_to([P, WIN, WIN, HEADS])
                nc.vector.tensor_tensor(prob[:, n % 2, :].rearrange("w (q k h) -> w q k h", q=POOL_QUERIES, k=WIN),
                                        by_key(e)[:, DVE_QUERIES:], by_q[:, DVE_QUERIES:],
                                        ALU.mult).then_inc(prob_done, 1)
                nc.vector.tensor_tensor(sm_ps[n % 2][:, PR].rearrange("w (q k h) -> w q k h", q=DVE_QUERIES, k=WIN),
                                        by_key(e)[:, 0:DVE_QUERIES], by_q[:, 0:DVE_QUERIES],
                                        ALU.mult).then_inc(prob_done, 1)

            def prob_value(n):
                dve.wait_ge(prob_done, 2 * (n + 1))
                dve.wait_ge(v_out, n + 1)
                if n >= 2:
                    dve.wait_ge(ot_made, n - 1)
                rows = WIN * HEADS
                o = pv[:, n % 2, :].rearrange("w (q kh d) -> w q kh d", q=WIN, d=HD)[:, 0:DVE_QUERIES]
                p = sm_ps[n % 2][:, PR].rearrange("w (q kh) -> w q kh", q=DVE_QUERIES)
                v = v_sb[:, n % 2, :].rearrange("w (kh d) -> w kh d", d=HD)
                nc.vector.tensor_tensor(o, p.unsqueeze(3).broadcast_to([P, DVE_QUERIES, rows, HD]),
                                        v.unsqueeze(1).broadcast_to([P, DVE_QUERIES, rows, HD]),
                                        ALU.mult).then_inc(pv_dve, 1)

            def result(n):
                b, half = TILES[n]
                dve.wait_ge(job_made, JOBS.index(("out", n)) + 1)
                order = "f (c k) -> f k c"
                nc.vector.scalar_tensor_tensor(
                    out=out_sb[:, n, :].rearrange(order, k=K), in0=job_ps[:, :].rearrange("f (k c) -> f k c", k=K),
                    scalar=bias_p[:, 0:1], in1=x_sb[:, b, half * TOK:(half + 1) * TOK].rearrange(order, k=K),
                    op0=ALU.add, op1=ALU.add).then_inc(job_dve, 1)

            batch_stats(0)
            spread(0)
            variance(0)
            normalise(0)
            batch_stats(1)
            spread(1)
            variance(1)
            query_key(0)
            normalise(1)
            dve.wait_ge(bp_loaded, 16)
            for s in range(N + 1):
                if s < N:
                    shift(s)
                if s + 1 < N:
                    query_key(s + 1)
                if s < N:
                    divide(s)
                    prob_value(s)
                for job in LATE.get(s, []):
                    if job[0] == "out":
                        result(job[1])

        @block.tensor
        def _(pe):
            def job_begins(job):
                j = JOBS.index(job)
                if j:
                    after_reader(pe, JOBS[j - 1])

            def do_job(job):
                job_begins(job)
                kind = job[0]
                if kind == "mean":
                    b0, nb = STATS[job[1]]
                    pe.wait_ge(mv_done, b0 + nb)
                    ins = nc.tensor.matmul(job_ps[:, 0:2 * nb], group_mean[:, :],
                                           mv[:, b0:b0 + nb, :].rearrange("p b s -> p (b s)"), start=True, stop=True)
                elif kind == "var":
                    b0, nb = STATS[job[1]]
                    pe.wait_ge(dev2_done, job[1] + 1)
                    ins = nc.tensor.matmul(job_ps[:, 0:nb], group_mean[:, :], dev2[:, b0:b0 + nb], start=True,
                                           stop=True)
                elif kind == "xt":
                    _, b, half = job
                    pe.wait_ge(xn_done, b + 1)
                    for i in range(4):
                        k = 4 * half + i
                        ins = nc.tensor.matmul(job_full[:, i // 2, i % 2], xn[:, b, k * P:(k + 1) * P], ident_chan,
                                               is_transpose=True, start=True, stop=True, skip_group_check=True)
                elif kind == "lt":
                    g = job[1]
                    pe.wait_ge(pooled_done, 2 * (g + 1))
                    for i in range(2):
                        for k in range(KL):
                            ins = nc.tensor.matmul(job_pool[:, i, k], pooled[:, 2 * g + i, k * P:(k + 1) * P],
                                                   ident_pchan, is_transpose=True, start=True, stop=True,
                                                   skip_group_check=True)
                else:
                    n = job[1]
                    b, half = TILES[n]
                    low = POOLED[b // 2]
                    pe.wait_ge(ot_out, max(n, low) + 1)
                    nc.tensor.matmul(job_ps[:, :], wp_sb[:, :], ot[:, n, :], start=True, stop=True,
                                     skip_group_check=True)
                    lo = ot[:, low, :].rearrange("f (b l c) -> f b l c", b=2, l=KL)
                    for i, (k, l) in enumerate(BLOCKS):
                        ins = nc.tensor.matmul(job_ps[:, k * CH:(k + 1) * CH], resize_sb[:, i, :],
                                               lo[:, b % 2, l, half * CH:(half + 1) * CH], start=False,
                                               stop=True, skip_group_check=True)
                ins.then_inc(job_made, 1)

            def queries_keys(n):
                if n >= 2:
                    pe.wait_ge(qk_dve, n - 1)
                if n >= 1:
                    pe.wait_ge(kq_out, 2 * n)
                b, half = TILES[n]
                if b is None:
                    pe.wait_ge(job_act, ACT_JOBS.index(("lt", half)) + 1)
                else:
                    pe.wait_ge(job_act, ACT_JOBS.index(("xt", b, 1)) + 1)
                for a, bank in ((0, q_ps[n % 2]), (1, k_ps)):
                    nc.tensor.matmul(bank[:, :].rearrange("w (q f) -> w q f", q=WIN), ones3[:, :],
                                     bias_qk[:, a * C:(a + 1) * C].unsqueeze(1).broadcast_to([3, WIN, C]),
                                     start=True, stop=True, skip_group_check=True)
                for r in range(2):
                    for s in range(2):
                        at = (2 * r + s) * C
                        for a, bank in ((0, q_ps[n % 2]), (1, k_ps)):
                            ins = nc.tensor.matmul(bank[:, at:at + C], tokens(n, r, s), wqk[:, a, :], start=False,
                                                   stop=True, skip_group_check=True)
                ins.then_inc(qk_made, 1)

            def values(n):
                if n >= 1:
                    pe.wait_ge(v_out, n)
                for r in range(2):
                    for s in range(2):
                        at = (2 * r + s) * C
                        ins = nc.tensor.matmul(v_ps[:, at:at + C], tokens(n, r, s), w_sb[:, 2 * C:3 * C],
                                               start=True, stop=True, skip_group_check=True)
                ins.then_inc(v_made, 1)

            def sum_scores(n):
                pe.wait_ge(qk_dve, n + 1)
                pe.wait_ge(qk_pool, n + 1)
                if n >= 2:
                    pe.wait_ge(pv_dve, n - 1)
                for d in range(HD):
                    ins = nc.tensor.matmul(sm_ps[n % 2][:, ST], qk[:, n % 2, d * NS:(d + 1) * NS], ident[:, :], is_transpose=True,
                                           start=(d == 0), stop=(d == HD - 1))
                ins.then_inc(st_made, 1)

            def turn_scores(n):
                pe.wait_ge(st_out, n + 1)
                nc.tensor.transpose(sm_ps[n % 2][:, SC], st_sb[:, n % 2, :], ident[:, :]).then_inc(s_made, 1)

            def sum_values(n):
                pe.wait_ge(pv_dve, n + 1)
                pe.wait_ge(pv_pool, n + 1)
                if n >= 1:
                    pe.wait_ge(ot_out, n)
                dst, eye = (ot_pool, ident_pool) if TILES[n][0] is None else (ot_full, ident_full)
                pv_n = pv[:, n % 2, :].rearrange("w (q k f) -> w q k f", q=WIN, k=WIN)
                for r in range(2):
                    for s in range(2):
                        for k in range(WIN):
                            ins = nc.tensor.matmul(dst[:, s, r], pv_n[:, 2 * r + s, k], eye, is_transpose=True,
                                                   start=(k == 0), stop=(k == WIN - 1), skip_group_check=True)
                ins.then_inc(ot_made, 1)

            pe.wait_ge(consts_made, 2)
            for job in PROLOGUE:
                do_job(job)
            pe.wait_ge(wqk_made, 2)
            pe.wait_ge(bias_made, 1)
            queries_keys(0)
            pe.wait_ge(w_loaded, 16)
            values(0)
            for s in STEPS:
                if 0 <= s - 1:
                    sum_values(s - 1)
                if s == min(t for t in LATE if any(j[0] == "out" for j in LATE[t])):
                    pe.wait_ge(wp_loaded, 16)
                    pe.wait_ge(resize_loaded, 16)
                for job in EARLY.get(s, []):
                    do_job(job)
                if s + 2 < N:
                    queries_keys(s + 2)
                if 0 <= s + 1 < N:
                    sum_scores(s + 1)
                if s + 2 < N:
                    values(s + 2)
                if 0 <= s + 1 < N:
                    turn_scores(s + 1)
                for job in LATE.get(s, []):
                    do_job(job)


def kernel(**inputs):
    import concourse.bacc as bacc
    from concourse.bass_utils import run_bass_kernel_spmd

    nc = bacc.Bacc("TRN2", target_bir_lowering=False, num_devices=1)
    names = ["x", "L0_conv_Wqkv", "L0_conv_bqkv", "L0_conv_Wproj", "L0_conv_bproj"]
    arrays = {f"in_{name}": np.ascontiguousarray(inputs[name]) for name in names}
    arrays["in_resize"] = RESIZE
    args = [nc.dram_tensor(name, a.shape, F32, kind="ExternalInput").ap() for name, a in arrays.items()]
    args.append(nc.dram_tensor("out_0", (B, C, H, W), F32, kind="ExternalOutput").ap())
    conv_attention_kernel(nc, *args)
    r = run_bass_kernel_spmd(nc, [arrays], core_ids=[0])
    return r.results[0]["out_0"]
```

```python
from contextlib import ExitStack

import numpy as np

import concourse.bass as bass
from concourse import mybir

ALU = mybir.AluOpType
ACT = mybir.ActivationFunctionType
AX = mybir.AxisListType
F32 = mybir.dt.float32
BF16 = mybir.dt.bfloat16

B, C, H, W = 4, 128, 32, 32
PIX = H * W
P = 128
K = PIX // P
HEADS = 8
HD = C // HEADS
GROUP = 4
EPS = 1e-5
WIN = 4
TILE_W = 128
PAIRS = WIN * WIN
NS = PAIRS * HEADS
SCALE = HD ** -0.5
DVE_QUERIES = 3
POOL_QUERIES = WIN - DVE_QUERIES
VBUF = 3
HALVES = 2
CH = C // HALVES
TOK = CH * K
PH, PW = H // 2, W // 2
KL = PH * PW // P

TILES = [(0, 0), (0, 1), (1, 0), (None, 0), (1, 1), (None, 1), (2, 0), (2, 1), (3, 0), (3, 1)]
N = len(TILES)
POOLED = [n for n, t in enumerate(TILES) if t[0] is None]
FULL = [n for n, t in enumerate(TILES) if t[0] is not None]

STATS = [(0, 1), (1, 1), (2, 2)]

LAST = B - 1
STEPS = range(-1, N + 1)
MID = {-1: [("xt", 1, 0)], 2: [("xt", 2, 0)], 3: [("xt", 2, 1)], 4: [("xt", 3, 0)],
       5: [("xt", 3, 1)]}
LATE = {-1: [("mean", 2), ("xt", 1, 1), ("var", 2)], 0: [("lt", 0)], 2: [("lt", 1)], 4: [("out", 0, 0)], 5: [("out", 0, 1)],
        6: [("out", 1, 0)], 7: [("out", 1, 1)], 8: [("out", 2, 0)], 9: [("out", 2, 1), ("begin", LAST, 0), ("begin", LAST, 1)],
        10: [("end", LAST, 0), ("end", LAST, 1)]}
WARM = {0: 12, 2: 8}
PROLOGUE = [("mean", 0), ("var", 0), ("xt", 0, 0), ("xt", 0, 1), ("mean", 1), ("var", 1)]
JOBS = PROLOGUE + [j for s in STEPS for j in MID.get(s, []) + LATE.get(s, [])]


def jobs_of(kinds):
    return [j for j in JOBS if j[0] in kinds]


def resize_blocks():
    def blur(n, front):
        m = np.zeros((n, n))
        for i in range(n):
            other = (i - 1 if i else 1) if front else (i + 1 if i < n - 1 else n - 2)
            m[i, i] += 0.5
            m[i, other] += 0.5
        return m

    def double(n):
        m = np.zeros((2 * n, n))
        for i in range(n):
            m[2 * i, i] += 0.75
            m[2 * i, max(i - 1, 0)] += 0.25
            m[2 * i + 1, i] += 0.75
            m[2 * i + 1, min(i + 1, n - 1)] += 0.25
        return m

    up_y, up_x = double(PH), double(PW)
    r = np.kron(up_y @ blur(PH, True), up_x) + np.kron(up_y, up_x @ blur(PW, False))
    r = r.T.reshape(KL, P, K, P)
    used = [(k, l) for k in range(K) for l in range(KL) if r[l, :, k].any()]
    return used, np.stack([r[l, :, k] for k, l in used], 1).astype(np.float32)


def halved_scores(n):
    return n > 0


def halved_values(n):
    return n < N - 1


BLOCKS, RESIZE = resize_blocks()


def conv_attention_kernel(nc, x, w_qkv, b_qkv, w_proj, b_proj, resize, out):
    x_dram = x.rearrange("b c h w -> b c (h w)")
    out_dram = out.rearrange("b f h w -> b f (h w)")

    with ExitStack() as ctx:
        def sb(name, shape, dt=F32):
            return ctx.enter_context(nc.sbuf_tensor(name, shape, dt))

        def psum(name):
            return ctx.enter_context(nc.psum_tensor(name, [P, 512], F32))

        def sem(name):
            return ctx.enter_context(nc.semaphore(name))

        ident = sb("ident", [P, P])
        group_mean = sb("group_mean", [P, P])
        ones3 = sb("ones3", [3, P], BF16)
        half_pow = sb("half_pow", [P, B])
        w_sb = sb("w_sb", [P, 3 * C])
        wqk = sb("wqk", [P, 2, C])
        wp_sb = sb("wp_sb", [P, C])
        resize_sb = sb("resize_sb", [P, len(BLOCKS), P])
        bias3 = sb("bias3", [3, 2 * C])
        minus = sb("minus", [3, 2])
        part = sb("part", [3, 2, 2 * C], BF16)
        rest = sb("rest", [3, 2 * C])
        bias_qk = sb("bias_qk", [3, 2 * C], BF16)
        bias_v = sb("bias_v", [P, 1])
        bias_p = sb("bias_p", [P, 1])
        x_sb = sb("x_sb", [P, B, PIX])
        xn = sb("xn", [P, B, PIX])
        rows2 = sb("rows2", [P, B, H * PW])
        pooled = sb("pooled", [P, B, PH * PW])
        bn = sb("bn", [P, B, 2, 6])
        mv = sb("mv", [P, B, 2])
        gstat = sb("gstat", [P, B, 2])
        dev = sb("dev", [P, B])
        dev2 = sb("dev2", [P, B])
        gvar = sb("gvar", [P, B])
        rstd = sb("rstd", [P, B])
        xt = sb("xt", [P, B, K * C])
        lt = sb("lt", [P, 2, 2 * KL * C])
        ot = sb("ot", [P, N, 512])
        out_sb = sb("out_sb", [P, B, PIX])
        q_sb = sb("q_sb", [P, 2, POOL_QUERIES * C])
        k_sb = sb("k_sb", [P, 2, WIN * C])
        v_sb = sb("v_sb", [P, VBUF, WIN * C])
        qk = sb("qk", [P, 2, PAIRS * C])
        pv = sb("pv", [P, 2, PAIRS * C])
        st_sb = sb("st_sb", [P, 2, TILE_W])
        row_max = sb("row_max", [P, 2, WIN * HEADS])
        shifted = sb("shifted", [P, 2, NS])
        expd = sb("expd", [P, 2, NS])
        denom = sb("denom", [P, 2, WIN * HEADS])
        inv = sb("inv", [P, 2, WIN * HEADS])

        q_ps = [psum("q_ps0"), psum("q_ps1")]
        k_ps = psum("k_ps")
        v_ps = psum("v_ps")
        sm_ps = [psum("sm_ps0"), psum("sm_ps1")]
        ot_ps = psum("ot_ps")
        job_ps = psum("job_ps")
        ST, SC, PR = slice(0, TILE_W), slice(TILE_W, TILE_W + NS), slice(2 * NS, 3 * NS)

        x0_rest = sem("x0_rest")
        x_loaded = [sem(f"x_loaded{b}") for b in range(B)]
        w_loaded, bias_loaded, bv_loaded, bp_loaded, wp_loaded, resize_loaded = (
            sem("w_loaded"), sem("bias_loaded"), sem("bv_loaded"), sem("bp_loaded"), sem("wp_loaded"),
            sem("resize_loaded"))
        out_stored = sem("out_stored")
        consts_set, consts_made = sem("consts_set"), sem("consts_made")
        minus_made, bias_step, bias_made = sem("minus_made"), sem("bias_step"), sem("bias_made")
        wqk_made = sem("wqk_made")
        bn_done, mv_done, dev_done, dev2_done = (
            sem("bn_done"), sem("mv_done"), sem("dev_done"), sem("dev2_done"))
        rstd_done, xn_done, rows_done, pooled_done = sem("rstd_done"), sem("xn_done"), sem("rows_done"), sem("pooled_done")
        qk_made, kq_out, v_made, v_out = sem("qk_made"), sem("kq_out"), sem("v_made"), sem("v_out")
        qk_dve, qk_pool, st_made, st_out, s_made = (
            sem("qk_dve"), sem("qk_pool"), sem("st_made"), sem("st_out"), sem("s_made"))
        max_done, shift_done, exp_done, denom_done, inv_done, prob_done = (
            sem("max_done"), sem("shift_done"), sem("exp_done"), sem("denom_done"), sem("inv_done"), sem("prob_done"))
        pv_dve, qk_halved, pv_halved, ot_made, ot_out = (
            sem("pv_dve"), sem("qk_halved"), sem("pv_halved"), sem("ot_made"), sem("ot_out"))
        job_made, job_act, job_dve = sem("job_made"), sem("job_act"), sem("job_dve")

        OUT_FIRST = jobs_of(("out",))[0]
        ACT_JOBS = jobs_of(("xt", "lt"))
        DVE_JOBS = jobs_of(("mean", "var", "out", "begin", "end"))

        def bank(job):
            if job in ACT_JOBS:
                return ot_ps if job == ("xt", 0, 1) else v_ps
            return k_ps if job in (("begin", LAST, 1), ("end", LAST, 1)) else job_ps

        def job_read(eng, job):
            if job in ACT_JOBS:
                eng.wait_ge(job_act, ACT_JOBS.index(job) + 1)
            else:
                eng.wait_ge(job_dve, DVE_JOBS.index(job) + 1)

        xt_view = xt[:, :, :].rearrange("f b (r s T w) -> f b r s T w", r=2, s=2, T=2)
        xt_rows = xt[:, :, :].rearrange("f b (n g m) -> f b g n m", g=2, m=8)
        ot_full = ot_ps[:, :].rearrange("f (k2 s i r c4) -> f s r i k2 c4", k2=4, s=2, i=8, r=2)
        ident_full = ident[:, :].rearrange("p (a b c) -> p a b c", a=8, b=4)
        ident_chan = ident[:, :].rearrange("p (a b c) -> p a b c", a=16, b=2)
        lt_view = lt[:, :, :].rearrange("f g (r s w) -> f g r s w", r=2, s=2)
        job_pool = v_ps[:, :].rearrange("f (r s b i j) -> f b s i r j", r=2, s=2, b=2, i=8)
        ot_pool = ot_ps[:, :].rearrange("f (b s i r j) -> f s r b i j", b=2, s=2, i=8, r=2)
        ident_pool = ident[:, :].rearrange("p (a b c) -> p a b c", a=2, b=8)
        ident_pchan = ident[:, :].rearrange("p (a b c) -> p a b c", a=8, b=2)

        def tokens(n, r, s):
            b, half = TILES[n]
            return lt_view[:, half, r, s] if b is None else xt_view[:, b, r, s, half]

        def query_key_operands(n, query, queries, i):
            to = qk[:, n % 2, :].rearrange("w (d q k h) -> w q k d h", d=HD, q=WIN, k=WIN)[:, query]
            q = queries[:, i * C:(i + 1) * C].rearrange("w (d h) -> w d h", d=HD).unsqueeze(1)
            keys = k_sb[:, n % 2, :].rearrange("w (k d h) -> w k d h", k=WIN, d=HD)
            return to, q.broadcast_to([P, WIN, HD, HEADS]), keys

        block = ctx.enter_context(nc.Block())

        @block.sync
        def _(sp):
            for i in range(2):
                sp.dma_start(x_sb[:, 0, i * 512:(i + 1) * 512], x_dram[0, :, i * 512:(i + 1) * 512]).then_inc(
                    x_loaded[0] if i == 0 else x0_rest, 16)
            for b in range(1, B):
                sp.dma_start(x_sb[:, b, :], x_dram[b]).then_inc(x_loaded[b], 16)
            for b in range(B - 1):
                sp.wait_ge(job_dve, DVE_JOBS.index(("out", b, 1)) + 1)
                sp.dma_start(out_dram[b], out_sb[:, b, :]).then_inc(out_stored, 16)
            for t, job in enumerate((("begin", LAST, 1), ("end", LAST, 1))):
                sp.wait_ge(job_dve, DVE_JOBS.index(job) + 1)
                sp.dma_start(out_dram[LAST, :, t * TOK:(t + 1) * TOK],
                             out_sb[:, LAST, t * TOK:(t + 1) * TOK]).then_inc(out_stored, 16)
            sp.wait_ge(out_stored, 16 * (B + 1))

        @block.gpsimd
        def _(pool):
            nc.gpsimd.memset(ident[:, :], 0.0).then_inc(consts_set, 1)
            nc.gpsimd.memset(group_mean[:, :], 1.0 / GROUP).then_inc(consts_set, 1)
            nc.gpsimd.memset(half_pow[:, :], -0.5).then_inc(consts_set, 1)
            nc.gpsimd.memset(ones3[:, :], 1.0).then_inc(consts_set, 1)
            nc.gpsimd.memset(minus[:, :], -1.0).then_inc(consts_set, 1)
            pool.wait_ge(consts_set, 5)
            nc.gpsimd.affine_select(out=minus[:, :], in_=minus[:, :], compare_op=ALU.is_gt, fill=0.0, base=0,
                                    pattern=[[-1, 2]], channel_multiplier=1).then_inc(minus_made, 1)
            nc.gpsimd.affine_select(out=ident[:, :], in_=ident[:, :], compare_op=ALU.not_equal, fill=1.0, base=0,
                                    pattern=[[-1, P]], channel_multiplier=1).then_inc(consts_made, 1)
            gm = group_mean[:, :].rearrange("p (g c) -> p g c", c=GROUP)
            nc.gpsimd.affine_select(out=gm, in_=gm, compare_op=ALU.is_ge, fill=0.0, base=0,
                                    pattern=[[-GROUP, P // GROUP], [0, GROUP]],
                                    channel_multiplier=1).then_inc(consts_set, 1)
            pool.wait_ge(consts_set, 6)
            nc.gpsimd.affine_select(out=gm, in_=gm, compare_op=ALU.is_ge, fill=0.0, base=GROUP - 1,
                                    pattern=[[GROUP, P // GROUP], [0, GROUP]],
                                    channel_multiplier=-1).then_inc(consts_made, 1)
            def inverse_std(g):
                b0, nb = STATS[g]
                pool.wait_ge(job_dve, DVE_JOBS.index(("var", g)) + 1)
                nc.gpsimd.tensor_tensor(rstd[:, b0:b0 + nb], gvar[:, b0:b0 + nb], half_pow[:, b0:b0 + nb],
                                        ALU.pow).then_inc(rstd_done, 1)

            def average_pool(b):
                pool.wait_ge(xn_done, b + 1)
                pix = xn[:, b, :].rearrange("c (y x s) -> c s y x", s=2, x=PW)
                nc.gpsimd.tensor_tensor(rows2[:, b, :].rearrange("c (y x) -> c y x", x=PW), pix[:, 0], pix[:, 1],
                                        ALU.add).then_inc(rows_done, 1)
                pool.wait_ge(rows_done, b + 1)
                row = rows2[:, b, :].rearrange("c (y s x) -> c s y x", s=2, x=PW)
                nc.gpsimd.tensor_tensor(pooled[:, b, :].rearrange("c (y x) -> c y x", x=PW), row[:, 0], row[:, 1],
                                        ALU.add).then_inc(pooled_done, 1)

            def query_key(n):
                pool.wait_ge(kq_out, 2 * (n + 1))
                if n >= 2:
                    pool.wait_ge(st_made, n - 1)
                for i in range(POOL_QUERIES):
                    ins = nc.gpsimd.tensor_tensor(*query_key_operands(n, DVE_QUERIES + i, q_sb[:, n % 2, :], i),
                                                  ALU.mult)
                ins.then_inc(qk_pool, 1)

            def halve_scores(n):
                if not halved_scores(n):
                    return
                pool.wait_ge(qk_dve, n + 1)
                pool.wait_ge(qk_pool, n + 1)
                low, high = qk[:, n % 2, 0:HD // 2 * NS], qk[:, n % 2, HD // 2 * NS:]
                nc.gpsimd.tensor_tensor(low, low, high, ALU.add).then_inc(qk_halved, 1)

            def halve_values(n):
                if not halved_values(n):
                    return
                pool.wait_ge(pv_dve, n + 1)
                v = pv[:, n % 2, :].rearrange("w (q two kf) -> w q two kf", q=WIN, two=2)
                nc.gpsimd.tensor_tensor(v[:, :, 0], v[:, :, 0], v[:, :, 1], ALU.add).then_inc(pv_halved, 1)

            inverse_std(0)
            average_pool(0)
            inverse_std(1)
            query_key(0)
            average_pool(1)
            for s in range(-1, N):
                if s + 1 < N:
                    halve_scores(s + 1)
                if s + 2 < N:
                    query_key(s + 2)
                if s == 0:
                    inverse_std(2)
                if s in (1, 2):
                    average_pool(s + 1)
                if s >= 0:
                    halve_values(s)

        @block.scalar
        def _(act):
            act.dma_start(bias3[:, :], b_qkv[0:2 * C].unsqueeze(0).broadcast_to([3, 2 * C])).then_inc(bias_loaded, 16)
            act.dma_start(w_sb[:, :], w_qkv).then_inc(w_loaded, 16)
            act.dma_start(bias_v[:, :], b_qkv[2 * C:3 * C].rearrange("(p a) -> p a", a=1)).then_inc(bv_loaded, 16)
            act.dma_start(bias_p[:, :], b_proj.rearrange("(p a) -> p a", a=1)).then_inc(bp_loaded, 16)
            act.dma_start(wp_sb[:, :], w_proj).then_inc(wp_loaded, 16)
            act.dma_start(resize_sb[:, :, :], resize).then_inc(resize_loaded, 16)
            act.wait_ge(w_loaded, 16)
            for a in range(2):
                nc.scalar.copy(wqk[:, a, :].rearrange("c (d h) -> c d h", d=HD),
                               w_sb[:, a * C:(a + 1) * C].rearrange("c (h d) -> c d h", h=HEADS)).then_inc(wqk_made, 1)

            def read_job(job):
                act.wait_ge(job_made, JOBS.index(job) + 1)
                if job[0] == "xt":
                    _, b, half = job
                    nc.scalar.copy(xt_rows[:, b, half], bank(job)[:, :].rearrange("f (n m) -> f n m", m=8)
                                   ).then_inc(job_act, 1)
                else:
                    nc.scalar.mul(lt[:, job[1], :], bank(job)[:, :], 0.25).then_inc(job_act, 1)

            def queries_keys_out(n):
                act.wait_ge(qk_made, n + 1)
                if n >= 2:
                    act.wait_ge(qk_dve, n - 1)
                    act.wait_ge(qk_pool, n - 1)
                nc.scalar.copy(q_sb[:, n % 2, :], q_ps[n % 2][:, DVE_QUERIES * C:]).then_inc(kq_out, 1)
                nc.scalar.copy(k_sb[:, n % 2, :], k_ps[:, :]).then_inc(kq_out, 1)

            def values_out(n):
                act.wait_ge(v_made, n + 1)
                if n >= VBUF:
                    act.wait_ge(pv_dve, n - VBUF + 1)
                nc.scalar.copy(v_sb[:, n % VBUF, :], v_ps[:, :]).then_inc(v_out, 1)

            def scores_t_out(n):
                act.wait_ge(st_made, n + 1)
                if n >= 2:
                    act.wait_ge(s_made, n - 1)
                nc.scalar.copy(st_sb[:, n % 2, :], sm_ps[n % 2][:, ST]).then_inc(st_out, 1)

            def exponent(n):
                act.wait_ge(shift_done, n + 1)
                if n >= 2:
                    act.wait_ge(prob_done, n - 1)
                nc.scalar.activation(expd[:, n % 2, :], shifted[:, n % 2, :], ACT.Exp, scale=SCALE).then_inc(exp_done, 1)

            def attention_out(n):
                act.wait_ge(ot_made, n + 1)
                nc.scalar.activation(ot[:, n, :], ot_ps[:, :], ACT.Identity, bias=bias_v[:, 0:1]).then_inc(ot_out, 1)

            for job in PROLOGUE:
                if job in ACT_JOBS:
                    read_job(job)
            act.wait_ge(bv_loaded, 16)
            queries_keys_out(0)
            values_out(0)
            for s in STEPS:
                if 0 <= s < N:
                    exponent(s)
                if s + 2 < N:
                    queries_keys_out(s + 2)
                if 0 <= s - 1:
                    attention_out(s - 1)
                if s + 2 < N:
                    values_out(s + 2)
                if 0 <= s + 1 < N:
                    scores_t_out(s + 1)
                for job in MID.get(s, []) + LATE.get(s, []):
                    if job in ACT_JOBS:
                        read_job(job)

        @block.vector
        def _(dve):
            def split_bias():
                dve.wait_ge(bias_loaded, 16)
                dve.wait_ge(minus_made, 1)
                nc.vector.tensor_copy(part[:, 0, :], bias3[:, :]).then_inc(bias_step, 1)
                dve.wait_ge(bias_step, 1)
                nc.vector.scalar_tensor_tensor(out=rest[:, :], in0=part[:, 0, :], scalar=minus[:, 0:1], in1=bias3[:, :],
                                               op0=ALU.mult, op1=ALU.add).then_inc(bias_step, 1)
                dve.wait_ge(bias_step, 2)
                nc.vector.tensor_copy(part[:, 1, :], rest[:, :]).then_inc(bias_step, 1)
                dve.wait_ge(bias_step, 3)
                order = "p (h d) -> p d h"
                for a in range(2):
                    at = slice(a * C, (a + 1) * C)
                    nc.vector.scalar_tensor_tensor(
                        out=bias_qk[:, at].rearrange("p (d h) -> p d h", d=HD),
                        in0=part[:, 1, at].rearrange(order, h=HEADS), scalar=minus[:, 1:2],
                        in1=rest[:, at].rearrange(order, h=HEADS), op0=ALU.mult, op1=ALU.add).then_inc(bias_made, 1)

            def batch_stats(g):
                b0, nb = STATS[g]
                for b in range(b0, b0 + nb):
                    dve.wait_ge(x_loaded[b], 16)
                    for i in range(2):
                        if b == 0 and i == 1:
                            dve.wait_ge(x0_rest, 16)
                        nc.vector.bn_stats(bn[:, b, i, :], x_sb[:, b, i * 512:(i + 1) * 512]).then_inc(bn_done, 1)
                for b in range(b0, b0 + nb):
                    dve.wait_ge(bn_done, 2 * (b + 1))
                    nc.vector.bn_aggr(mv[:, b, :], bn[:, b, :, :].rearrange("p i s -> p (i s)")).then_inc(mv_done, 1)

            def spread(g):
                b0, nb = STATS[g]
                bs = slice(b0, b0 + nb)
                dve.wait_ge(job_made, JOBS.index(("mean", g)) + 1)
                dve.wait_ge(mv_done, b0 + nb)
                m = job_ps[:, 0:2 * nb].rearrange("p (b s) -> p b s", s=2)
                nc.vector.tensor_tensor(dev[:, bs], mv[:, bs, 0], m[:, :, 0], ALU.subtract).then_inc(dev_done, 1)
                nc.vector.tensor_copy(gstat[:, bs, :], m).then_inc(job_dve, 1)
                dve.wait_ge(dev_done, g + 1)
                nc.vector.tensor_tensor(dev2[:, bs], dev[:, bs], dev[:, bs], ALU.mult).then_inc(dev2_done, 1)

            def variance(g):
                b0, nb = STATS[g]
                bs = slice(b0, b0 + nb)
                dve.wait_ge(job_made, JOBS.index(("var", g)) + 1)
                dve.wait_ge(job_dve, DVE_JOBS.index(("mean", g)) + 1)
                nc.vector.scalar_tensor_tensor(out=gvar[:, bs], in0=job_ps[:, 0:nb], scalar=EPS, in1=gstat[:, bs, 1],
                                               op0=ALU.add, op1=ALU.add).then_inc(job_dve, 1)

            def normalise(b):
                dve.wait_ge(rstd_done, 1 + min(b, 2))
                nc.vector.tensor_scalar(xn[:, b, :], x_sb[:, b, :], gstat[:, b, 0:1], rstd[:, b:b + 1],
                                        ALU.subtract, ALU.mult).then_inc(xn_done, 1)

            def query_key(n):
                dve.wait_ge(kq_out, 2 * (n + 1))
                if n >= 2:
                    dve.wait_ge(st_made, n - 1)
                for i in range(DVE_QUERIES):
                    ins = nc.vector.tensor_tensor(*query_key_operands(n, i, q_ps[n % 2][:, :], i), ALU.mult)
                ins.then_inc(qk_dve, 1)

            def by_key(ap):
                return ap.rearrange("w (q k h) -> w q k h", q=WIN, k=WIN)

            def by_head(ap):
                return ap.rearrange("w (q h) -> w q h", q=WIN)

            def shift(n):
                dve.wait_ge(s_made, n + 1)
                sc = sm_ps[n % 2][:, SC]
                nc.vector.tensor_reduce(by_head(row_max[:, n % 2, :]),
                                        sc.rearrange("w (q k h) -> w q h k", q=WIN, k=WIN), AX.X,
                                        ALU.max).then_inc(max_done, 1)
                dve.wait_ge(max_done, n + 1)
                if n >= 2:
                    dve.wait_ge(exp_done, n - 1)
                nc.vector.tensor_tensor(by_key(shifted[:, n % 2, :]), by_key(sc),
                                        by_head(row_max[:, n % 2, :]).unsqueeze(2).broadcast_to([P, WIN, WIN, HEADS]),
                                        ALU.subtract).then_inc(shift_done, 1)

            def divide(n):
                dve.wait_ge(exp_done, n + 1)
                e = expd[:, n % 2, :]
                nc.vector.tensor_reduce(by_head(denom[:, n % 2, :]),
                                        e.rearrange("w (q k h) -> w q h k", q=WIN, k=WIN), AX.X,
                                        ALU.add).then_inc(denom_done, 1)
                dve.wait_ge(denom_done, n + 1)
                nc.vector.reciprocal(inv[:, n % 2, :], denom[:, n % 2, :]).then_inc(inv_done, 1)
                dve.wait_ge(inv_done, n + 1)
                nc.vector.tensor_tensor(by_key(sm_ps[n % 2][:, PR]), by_key(e),
                                        by_head(inv[:, n % 2, :]).unsqueeze(2).broadcast_to([P, WIN, WIN, HEADS]),
                                        ALU.mult).then_inc(prob_done, 1)

            def prob_value(n):
                dve.wait_ge(prob_done, n + 1)
                dve.wait_ge(v_out, n + 1)
                if n >= 2:
                    dve.wait_ge(ot_made, n - 1)
                shape = [P, WIN, WIN * HEADS, HD]
                p = sm_ps[n % 2][:, PR].rearrange("w (q kh) -> w q kh", q=WIN)
                v = v_sb[:, n % VBUF, :].rearrange("w (kh d) -> w kh d", d=HD)
                nc.vector.tensor_tensor(pv[:, n % 2, :].rearrange("w (q kh d) -> w q kh d", q=WIN, d=HD),
                                        p.unsqueeze(3).broadcast_to(shape), v.unsqueeze(1).broadcast_to(shape),
                                        ALU.mult).then_inc(pv_dve, 1)

            def result(job):
                kind, b, half = job
                cs = {"out": slice(0, C), "begin": slice(0, CH), "end": slice(CH, C)}[kind]
                ks = slice(half * K // 2, (half + 1) * K // 2)
                dve.wait_ge(job_made, JOBS.index(job) + 1)
                nc.vector.scalar_tensor_tensor(
                    out=out_sb[:, b, :].rearrange("f (c k) -> f c k", k=K)[:, cs, ks],
                    in0=bank(job)[:, :].rearrange("f (k c) -> f c k", c=C)[:, cs], scalar=bias_p[:, 0:1],
                    in1=x_sb[:, b, :].rearrange("f (c k) -> f c k", k=K)[:, cs, ks],
                    op0=ALU.add, op1=ALU.add).then_inc(job_dve, 1)

            def results(s):
                for job in LATE.get(s, []):
                    if job[0] in ("out", "begin", "end"):
                        result(job)

            for g in range(2):
                batch_stats(g)
                spread(g)
                variance(g)
                normalise(g)
                if g == 0:
                    split_bias()
            query_key(0)
            batch_stats(2)
            dve.wait_ge(bp_loaded, 16)
            for s in range(N + 1):
                if s == 0:
                    spread(2)
                if s < N:
                    shift(s)
                if s + 1 < N:
                    query_key(s + 1)
                if s == 0:
                    variance(2)
                if s == 1:
                    normalise(2)
                    normalise(3)
                results(s - 1)
                if s < N:
                    divide(s)
                    prob_value(s)
            results(N)

        @block.tensor
        def _(pe):
            def job_begins(job):
                earlier = [j for j in JOBS[:JOBS.index(job)] if bank(j) is bank(job)]
                if earlier:
                    job_read(pe, earlier[-1])

            def do_job(job, values_before=0):
                job_begins(job)
                if values_before and bank(job) is v_ps:
                    pe.wait_ge(v_out, values_before)
                kind = job[0]
                if kind == "mean":
                    b0, nb = STATS[job[1]]
                    pe.wait_ge(mv_done, b0 + nb)
                    ins = nc.tensor.matmul(job_ps[:, 0:2 * nb], group_mean[:, :],
                                           mv[:, b0:b0 + nb, :].rearrange("p b s -> p (b s)"), start=True, stop=True)
                elif kind == "var":
                    b0, nb = STATS[job[1]]
                    pe.wait_ge(dev2_done, job[1] + 1)
                    ins = nc.tensor.matmul(job_ps[:, 0:nb], group_mean[:, :], dev2[:, b0:b0 + nb], start=True,
                                           stop=True)
                elif kind == "xt":
                    _, b, half = job
                    pe.wait_ge(xn_done, b + 1)
                    to = bank(job)[:, :].rearrange("f (r s n k2 c4) -> f k2 s n r c4", r=2, s=2, n=16, k2=2)
                    for i in range(4):
                        k = 4 * half + i
                        ins = nc.tensor.matmul(to[:, i // 2, i % 2], xn[:, b, k * P:(k + 1) * P], ident_chan,
                                               is_transpose=True, start=True, stop=True, skip_group_check=True)
                elif kind == "lt":
                    g = job[1]
                    pe.wait_ge(pooled_done, 2 * (g + 1))
                    for i in range(2):
                        for k in range(KL):
                            ins = nc.tensor.matmul(job_pool[:, i, k], pooled[:, 2 * g + i, k * P:(k + 1) * P],
                                                   ident_pchan, is_transpose=True, start=True, stop=True,
                                                   skip_group_check=True)
                else:
                    _, b, half = job
                    low = POOLED[b // 2]
                    tiles = [TILES.index((b, t)) for t in range(HALVES)]
                    if kind != "end":
                        blocks = [i for i, (k, _) in enumerate(BLOCKS) if k // (K // 2) == half]
                        pe.wait_ge(ot_out, low + 1)
                        for i in blocks:
                            k, l = BLOCKS[i]
                            at = (k - half * K // 2) * C
                            low_ot = ot[:, low, :].rearrange("f (b l c) -> f b l c", b=2, l=KL)[:, b % 2, l]
                            ins = nc.tensor.matmul(bank(job)[:, at:at + C], resize_sb[:, i, :], low_ot,
                                                   start=(i == blocks[0]), stop=True, skip_group_check=True)
                    for t in {"out": (0, 1), "begin": (0,), "end": (1,)}[kind]:
                        pe.wait_ge(ot_out, tiles[t] + 1)
                        ins = nc.tensor.matmul(
                            bank(job)[:, :].rearrange("f (k t c) -> f t k c", t=HALVES, c=CH)[:, t], wp_sb[:, :],
                            ot[:, tiles[t], :].rearrange("f (h k c) -> f h k c", h=2, c=CH)[:, half],
                            start=False, stop=True, skip_group_check=True)
                ins.then_inc(job_made, 1)

            def queries_keys(n, job_between=None):
                if n >= 2:
                    pe.wait_ge(qk_dve, n - 1)
                if n >= 1:
                    pe.wait_ge(kq_out, 2 * n)
                b, half = TILES[n]
                if b is None:
                    pe.wait_ge(job_act, ACT_JOBS.index(("lt", half)) + 1)
                else:
                    pe.wait_ge(job_act, ACT_JOBS.index(("xt", b, 1)) + 1)
                for a, to in ((0, q_ps[n % 2]), (1, k_ps)):
                    nc.tensor.matmul(to[:, :].rearrange("w (q f) -> w q f", q=WIN), ones3[:, :],
                                     bias_qk[:, a * C:(a + 1) * C].unsqueeze(1).broadcast_to([3, WIN, C]),
                                     start=True, stop=True, skip_group_check=True)
                for r in range(2):
                    if r and job_between:
                        do_job(job_between)
                    for s in range(2):
                        at = (2 * r + s) * C
                        for a, to in ((0, q_ps[n % 2]), (1, k_ps)):
                            ins = nc.tensor.matmul(to[:, at:at + C], tokens(n, r, s), wqk[:, a, :], start=False,
                                                   stop=True, skip_group_check=True)
                ins.then_inc(qk_made, 1)

            def values(n, jobs_before):
                if n >= 1:
                    pe.wait_ge(v_out, n)
                if jobs_before:
                    pe.wait_ge(job_act, jobs_before)
                for r in range(2):
                    for s in range(2):
                        at = (2 * r + s) * C
                        ins = nc.tensor.matmul(v_ps[:, at:at + C], tokens(n, r, s), w_sb[:, 2 * C:3 * C],
                                               start=True, stop=True, skip_group_check=True)
                ins.then_inc(v_made, 1)

            def sum_scores(n):
                if halved_scores(n):
                    pe.wait_ge(qk_halved, sum(map(halved_scores, range(n + 1))))
                else:
                    pe.wait_ge(qk_dve, n + 1)
                    pe.wait_ge(qk_pool, n + 1)
                terms = HD // 2 if halved_scores(n) else HD
                if n >= 2:
                    pe.wait_ge(pv_dve, n - 1)
                for d in range(terms):
                    ins = nc.tensor.matmul(sm_ps[n % 2][:, ST], qk[:, n % 2, d * NS:(d + 1) * NS], ident[:, :], is_transpose=True,
                                           start=(d == 0), stop=(d == terms - 1))
                ins.then_inc(st_made, 1)

            def turn_scores(n):
                pe.wait_ge(st_out, n + 1)
                nc.tensor.transpose(sm_ps[n % 2][:, SC], st_sb[:, n % 2, :], ident[:, :]).then_inc(s_made, 1)

            def sum_values(n):
                if halved_values(n):
                    pe.wait_ge(pv_halved, sum(map(halved_values, range(n + 1))))
                else:
                    pe.wait_ge(pv_dve, n + 1)
                terms = WIN // 2 if halved_values(n) else WIN
                if n >= 1:
                    pe.wait_ge(ot_out, n)
                dst, eye = (ot_pool, ident_pool) if TILES[n][0] is None else (ot_full, ident_full)
                pv_n = pv[:, n % 2, :].rearrange("w (q k f) -> w q k f", q=WIN, k=WIN)
                for r in range(2):
                    for s in range(2):
                        for k in range(terms):
                            ins = nc.tensor.matmul(dst[:, s, r], pv_n[:, 2 * r + s, k], eye, is_transpose=True,
                                                   start=(k == 0), stop=(k == terms - 1), skip_group_check=True)
                ins.then_inc(ot_made, 1)

            def keep_warm(n):
                for _ in range(n):
                    nc.tensor.transpose(sm_ps[1][:, ST], ident[:, :], ident[:, :])

            pe.wait_ge(consts_made, 2)
            for n, job in enumerate(PROLOGUE[:4]):
                if n in WARM:
                    keep_warm(WARM[n])
                do_job(job)
            pe.wait_ge(wqk_made, 2)
            pe.wait_ge(bias_made, 2)
            keep_warm(4)
            queries_keys(0, PROLOGUE[4])
            do_job(PROLOGUE[5])
            pe.wait_ge(w_loaded, 16)
            values(0, 0)
            turned = 2
            for s in STEPS:
                if s + 2 < N:
                    queries_keys(s + 2)
                if 0 <= s - 1:
                    sum_values(s - 1)
                if s + 2 < N:
                    values(s + 2, turned)
                if 0 <= s + 1 < N:
                    sum_scores(s + 1)
                for job in MID.get(s, []):
                    do_job(job, min(s + 3, N))
                if 0 <= s + 1 < N:
                    turn_scores(s + 1)
                for job in LATE.get(s, []):
                    if job == OUT_FIRST:
                        pe.wait_ge(wp_loaded, 16)
                        pe.wait_ge(resize_loaded, 16)
                    do_job(job, min(s + 3, N))
                turned += sum(job in ACT_JOBS for job in MID.get(s, []) + LATE.get(s, []))


def kernel(**inputs):
    import concourse.bacc as bacc
    from concourse.bass_utils import run_bass_kernel_spmd

    nc = bacc.Bacc("TRN2", target_bir_lowering=False, num_devices=1)
    names = ["x", "L0_conv_Wqkv", "L0_conv_bqkv", "L0_conv_Wproj", "L0_conv_bproj"]
    arrays = {f"in_{name}": np.ascontiguousarray(inputs[name]) for name in names}
    arrays["in_resize"] = RESIZE
    args = [nc.dram_tensor(name, a.shape, F32, kind="ExternalInput").ap() for name, a in arrays.items()]
    args.append(nc.dram_tensor("out_0", (B, C, H, W), F32, kind="ExternalOutput").ap())
    conv_attention_kernel(nc, *args)
    r = run_bass_kernel_spmd(nc, [arrays], core_ids=[0])
    return r.results[0]["out_0"]
```

```python
from contextlib import ExitStack

import numpy as np

import concourse.bass as bass
from concourse import mybir

ALU = mybir.AluOpType
ACT = mybir.ActivationFunctionType
AX = mybir.AxisListType
F32 = mybir.dt.float32
BF16 = mybir.dt.bfloat16

B, C, H, W = 4, 128, 32, 32
PIX = H * W
P = 128
K = PIX // P
HEADS = 8
HD = C // HEADS
GROUP = 4
EPS = 1e-5
WIN = 4
TILE_W = 128
PAIRS = WIN * WIN
NS = PAIRS * HEADS
SCALE = HD ** -0.5
POOL_QUERIES = 2
VBUF = 3
HALVES = 2
CH = C // HALVES
TOK = CH * K
PH, PW = H // 2, W // 2
KL = PH * PW // P

TILES = [(0, 0), (0, 1), (None, 0), (1, 0), (1, 1), (2, 0), (None, 1), (2, 1), (3, 0), (3, 1)]
N = len(TILES)
POOLED = [n for n, t in enumerate(TILES) if t[0] is None]

STATS = [(0, 1), (1, 1), (2, 2)]

LAST = B - 1


def resize_blocks():
    def blur(n, front):
        m = np.zeros((n, n))
        for i in range(n):
            other = (i - 1 if i else 1) if front else (i + 1 if i < n - 1 else n - 2)
            m[i, i] += 0.5
            m[i, other] += 0.5
        return m

    def double(n):
        m = np.zeros((2 * n, n))
        for i in range(n):
            m[2 * i, i] += 0.75
            m[2 * i, max(i - 1, 0)] += 0.25
            m[2 * i + 1, i] += 0.75
            m[2 * i + 1, min(i + 1, n - 1)] += 0.25
        return m

    up_y, up_x = double(PH), double(PW)
    r = np.kron(up_y @ blur(PH, True), up_x) + np.kron(up_y, up_x @ blur(PW, False))
    r = r.T.reshape(KL, P, K, P)
    used = [(k, l) for k in range(K) for l in range(KL) if r[l, :, k].any()]
    return used, np.stack([r[l, :, k] for k, l in used], 1).astype(np.float32)


BLOCKS, RESIZE = resize_blocks()

ORDER = {
    "PE": [
        ("mean", 0), ("var", 0), ("mix",), ("xt", 0, 0), ("xt", 0, 1), ("K", 0), ("mean", 1), ("Q", 0), ("var", 1),
        ("K", 1), ("Q", 1), ("V", 0), ("S", 0), ("T", 0), ("lt", 0), ("V", 1), ("K", 2), ("Q", 2), ("xt", 1, 1),
        ("S", 1), ("V", 2), ("xt", 1, 0), ("T", 1), ("mean", 2), ("var", 2), ("K", 3), ("Q", 3), ("V", 3), ("O", 0),
        ("Q", 4), ("S", 2), ("T", 2), ("K", 4), ("xt", 2, 0), ("O", 1), ("S", 3), ("xt", 2, 1), ("T", 3), ("V", 4),
        ("Q", 5), ("K", 5), ("O", 2), ("lt", 1), ("S", 4), ("V", 5), ("T", 4), ("Q", 6), ("K", 6), ("out", 0, 0),
        ("O", 3), ("S", 5), ("V", 6), ("Q", 7), ("T", 5), ("K", 7), ("out", 0, 1), ("O", 4), ("xt", 3, 0), ("S", 6),
        ("V", 7), ("xt", 3, 1), ("T", 6), ("out", 1, 0), ("K", 8), ("Q", 8), ("S", 7), ("V", 8), ("T", 7), ("O", 5),
        ("K", 9), ("out", 1, 1), ("Q", 9), ("O", 6), ("S", 8), ("V", 9), ("T", 8), ("low", 3, 0), ("O", 7),
        ("S", 9), ("low", 3, 1), ("T", 9), ("out", 2, 0), ("O", 8), ("out", 2, 1), ("O", 9), ("begin", 3, 0),
        ("begin", 3, 1), ("end", 3, 0), ("end", 3, 1),
    ],
    "ACT": [
        ("bias",), ("SK", 0), ("SQ", 0), ("wqk_mix",), ("xt", 0, 0), ("xt", 0, 1), ("K", 0), ("SK", 1), ("Q", 0),
        ("SQ", 1), ("K", 1), ("SK", 2), ("SQ", 2), ("Q", 1), ("V", 0), ("wqk",), ("S", 0), ("X", 0), ("lt", 0),
        ("V", 1), ("K", 2), ("SK", 3), ("Q", 2), ("xt", 1, 1), ("SQ", 3), ("S", 1), ("xt", 1, 0), ("V", 2),
        ("X", 1), ("K", 3), ("SK", 4), ("Q", 3), ("SQ", 4), ("norm", 2, 0), ("norm", 2, 1), ("S", 2), ("V", 3),
        ("X", 2), ("O", 0), ("K", 4), ("SK", 5), ("xt", 2, 0), ("Q", 4), ("O", 1), ("SQ", 5), ("S", 3),
        ("xt", 2, 1), ("X", 3), ("V", 4), ("O", 2), ("K", 5), ("Q", 5), ("lt", 1), ("SQ", 6), ("S", 4), ("SK", 6),
        ("X", 4), ("Q", 6), ("V", 5), ("K", 6), ("SK", 7), ("O", 3), ("SQ", 7), ("S", 5), ("X", 5), ("K", 7),
        ("V", 6), ("SQ", 8), ("Q", 7), ("SK", 8), ("O", 4), ("xt", 3, 0), ("S", 6), ("V", 7), ("xt", 3, 1),
        ("X", 6), ("K", 8), ("SQ", 9), ("SK", 9), ("Q", 8), ("S", 7), ("X", 7), ("O", 5), ("Q", 9), ("K", 9),
        ("V", 8), ("S", 8), ("O", 6), ("V", 9), ("X", 8), ("S", 9), ("O", 7), ("X", 9), ("O", 8), ("O", 9),
    ],
    "DVE": [
        ("bn", 0), ("mean", 0), ("var", 0), ("norm", 0, 1), ("norm", 0, 0), ("bn", 1), ("mean", 1), ("var", 1),
        ("M", 0, 0), ("M", 0, 1), ("M", 0, 2), ("norm", 1, 1), ("norm", 1, 0), ("bn", 2), ("M", 1, 0), ("M", 1, 1),
        ("X", 0), ("bn", 3), ("D", 0), ("P", 0), ("M", 2, 0), ("M", 2, 1), ("mean", 2), ("X", 1), ("var", 2),
        ("M", 2, 2), ("D", 1), ("P", 1), ("M", 3, 0), ("norm", 3, 1), ("M", 3, 1), ("norm", 3, 0), ("X", 2),
        ("M", 3, 2), ("D", 2), ("P", 2), ("M", 4, 0), ("M", 4, 1), ("M", 4, 2), ("X", 3), ("D", 3), ("P", 3),
        ("M", 5, 0), ("M", 5, 1), ("M", 5, 2), ("X", 4), ("M", 5, 3), ("D", 4), ("P", 4), ("M", 6, 0),
        ("out", 0, 0), ("M", 6, 1), ("M", 6, 2), ("X", 5), ("M", 6, 3), ("D", 5), ("P", 5), ("out", 0, 1),
        ("M", 7, 0), ("M", 7, 1), ("X", 6), ("M", 7, 2), ("D", 6), ("M", 7, 3), ("out", 1, 0), ("P", 6),
        ("M", 8, 0), ("M", 8, 1), ("X", 7), ("M", 8, 2), ("D", 7), ("P", 7), ("M", 9, 0), ("M", 9, 1),
        ("out", 1, 1), ("X", 8), ("M", 9, 2), ("D", 8), ("P", 8), ("HV", 8), ("X", 9), ("D", 9), ("out", 2, 0),
        ("P", 9), ("out", 2, 1), ("begin", 3, 0), ("begin", 3, 1), ("end", 3, 0), ("end", 3, 1),
    ],
    "POOL": [
        ("std", 0), ("std", 1), ("M", 0, 3), ("M", 1, 2), ("M", 1, 3), ("HS", 1), ("HS2", 1), ("M", 2, 3),
        ("HV", 0), ("std", 2), ("HS", 2), ("M", 3, 3), ("M", 4, 3), ("HV", 2), ("HV2", 2), ("HS", 4), ("HV", 3),
        ("HV2", 3), ("HS", 5), ("HV", 4), ("HV2", 4), ("HS", 6), ("HV", 5), ("HV2", 5), ("M", 8, 3), ("HV", 6),
        ("HS", 8), ("HV", 7), ("M", 9, 3),
    ],
}
V_BANK_JOBS = [("xt", 0, 0), ("lt", 1), ("xt", 2, 0), ("xt", 3, 0)]
WARM = {("mean", 0): 7, ("var", 0): 1, ("xt", 0, 0): 0, ("K", 0): 0}


def conv_attention_kernel(nc, x, w_qkv, b_qkv, w_proj, b_proj, resize, out):
    x_dram = x.rearrange("b c h w -> b c (h w)")
    out_dram = out.rearrange("b f h w -> b f (h w)")

    with ExitStack() as ctx:
        def sb(name, shape, dt=F32):
            return ctx.enter_context(nc.sbuf_tensor(name, shape, dt))

        def psum(name):
            return ctx.enter_context(nc.psum_tensor(name, [P, 512], F32))

        def sem(name):
            return ctx.enter_context(nc.semaphore(name))

        ident = sb("ident", [P, P])
        group_mean = sb("group_mean", [P, P])
        ones3 = sb("ones3", [3, P], BF16)
        half_pow = sb("half_pow", [P, B])
        w_sb = sb("w_sb", [P, 3 * C])
        wqk = sb("wqk", [P, 2, C])
        wv_mix = sb("wv_mix", [P, C])
        mixer = sb("mixer", [P, P])
        wqk_mix = sb("wqk_mix", [P, 2, C])
        wp_sb = sb("wp_sb", [P, C])
        resize_sb = sb("resize_sb", [P, len(BLOCKS), P])
        bias_rows = sb("bias_rows", [P, 2 * C])
        bias_qk = sb("bias_qk", [P, 2, C])
        bias_v = sb("bias_v", [P, 1])
        bias_p = sb("bias_p", [P, 1])
        x_sb = sb("x_sb", [P, B, PIX])
        xn = sb("xn", [P, B, PIX])
        bn = sb("bn", [P, B, 2, 6])
        mv = sb("mv", [P, B, 2])
        gstat = sb("gstat", [P, B, 2])
        dev = sb("dev", [P, B])
        dev2 = sb("dev2", [P, B])
        gvar = sb("gvar", [P, B])
        rstd = sb("rstd", [P, B])
        neg_mean = sb("neg_mean", [P, B])
        offset = sb("offset", [P, B])
        xt = sb("xt", [P, B, K * C])
        lt = sb("lt", [P, 2, 2 * KL * C])
        ot = sb("ot", [P, N, 512])
        out_sb = sb("out_sb", [P, B, PIX])
        q_sb = sb("q_sb", [P, 2, POOL_QUERIES * C])
        k_sb = sb("k_sb", [P, 2, WIN * C])
        v_sb = sb("v_sb", [P, VBUF, WIN * C])
        qk = sb("qk", [P, 2, PAIRS * C])
        pv = sb("pv", [P, 2, PAIRS * C])
        st_sb = sb("st_sb", [P, 2, TILE_W])
        row_max = sb("row_max", [P, 2, WIN * HEADS])
        shifted = sb("shifted", [P, 2, NS])
        expd = sb("expd", [P, 2, NS])
        denom = sb("denom", [P, 2, WIN * HEADS])
        inv = sb("inv", [P, 2, WIN * HEADS])

        q_ps = [psum("q_ps0"), psum("q_ps1")]
        k_ps = psum("k_ps")
        v_ps = psum("v_ps")
        sm_ps = [psum("sm_ps0"), psum("sm_ps1")]
        ot_ps = psum("ot_ps")
        job_ps = psum("job_ps")
        ST, SC, PR = slice(0, TILE_W), slice(TILE_W, TILE_W + NS), slice(2 * NS, 3 * NS)

        x0_rest = sem("x0_rest")
        x_loaded = [sem(f"x_loaded{b}") for b in range(B)]
        w_loaded, bias_loaded, bv_loaded, bp_loaded, wp_loaded, resize_loaded, mix_made = (
            sem("w_loaded"), sem("bias_loaded"), sem("bv_loaded"), sem("bp_loaded"), sem("wp_loaded"),
            sem("resize_loaded"), sem("mix_made"))
        out_stored = sem("out_stored")
        consts_set, consts_made = sem("consts_set"), sem("consts_made")
        bias_made, bits_set, k_seeded, q_seeded = sem("bias_made"), sem("bits_set"), sem("k_seeded"), sem("q_seeded")
        wqk_made = sem("wqk_made")
        mixer_made = sem("mixer_made")
        bn_done, mv_done, dev_done, dev2_done = (
            sem("bn_done"), sem("mv_done"), sem("dev_done"), sem("dev2_done"))
        rstd_done, neg_done, offset_done = sem("rstd_done"), sem("neg_done"), sem("offset_done")
        xn_dve, xn_act = sem("xn_dve"), sem("xn_act")
        k_made, q_made, k_out, q_out, v_made, v_out = (
            sem("k_made"), sem("q_made"), sem("k_out"), sem("q_out"), sem("v_made"), sem("v_out"))
        qk_dve, qk_pool, st_made, st_out, s_made = (
            sem("qk_dve"), sem("qk_pool"), sem("st_made"), sem("st_out"), sem("s_made"))
        max_done, shift_done, exp_done, denom_done, inv_done, prob_done = (
            sem("max_done"), sem("shift_done"), sem("exp_done"), sem("denom_done"), sem("inv_done"), sem("prob_done"))
        pv_dve, pv_last, ot_made, ot_out = (
            sem("pv_dve"), sem("pv_last"), sem("ot_made"), sem("ot_out"))
        halved_pool = {kind: sem(f"pool_{kind}") for kind in ("HS", "HS2", "HV", "HV2")}
        halved_dve = {kind: sem(f"dve_{kind}") for kind in ("HS", "HS2", "HV", "HV2")}
        job_made, job_act, job_dve = sem("job_made"), sem("job_act"), sem("job_dve")

        def among(order, kinds):
            return [j for j in order if j[0] in kinds]

        def before(order, job, kinds):
            return len(among(order[:order.index(job)], kinds))

        JOBS = among(ORDER["PE"], ("mean", "var", "xt", "lt", "out", "low", "begin", "end"))
        ACT_JOBS = among(ORDER["ACT"], ("xt", "lt"))
        DVE_JOBS = among(ORDER["DVE"], ("mean", "var", "out", "begin", "end"))
        NORMED = [among(ORDER[e], ("norm",)) for e in ("DVE", "ACT")]

        def tiles_done(engine, kind, n):
            return sum(job[0] == kind and job[1] <= n for job in ORDER[engine])

        def sums_halved(eng, kinds, n):
            times = 0
            for kind in kinds:
                for engine, done in (("POOL", halved_pool), ("DVE", halved_dve)):
                    if (kind, n) in ORDER[engine]:
                        eng.wait_ge(done[kind], tiles_done(engine, kind, n))
                        times += 1
            return times

        def products_done(eng, n):
            if n >= 0:
                eng.wait_ge(qk_dve, n + 1)
                if tiles_done("POOL", "M", n):
                    eng.wait_ge(qk_pool, tiles_done("POOL", "M", n))

        def normalised(b):
            for done, by in zip((xn_dve, xn_act), NORMED):
                if ("norm", b, 0) in by:
                    return done, max(by.index(("norm", b, y)) for y in range(2)) + 1

        def bank(job):
            if job[0] in ("xt", "lt"):
                return v_ps if job in V_BANK_JOBS else ot_ps
            if job == ("out", LAST - 1, 1):
                return k_ps
            if job[0] in ("low", "begin", "end"):
                return v_ps if job[2] else q_ps[0]
            return job_ps

        def job_read(eng, job):
            if job in ACT_JOBS:
                eng.wait_ge(job_act, ACT_JOBS.index(job) + 1)
            else:
                eng.wait_ge(job_dve, DVE_JOBS.index(job) + 1)

        xt_view = xt[:, :, :].rearrange("f b (r s T w) -> f b r s T w", r=2, s=2, T=2)
        xt_side = xt[:, :, :].rearrange("f b (r s m) -> f b s r m", r=2, s=2)
        ot_full = ot_ps[:, :].rearrange("f (k2 s i r c4) -> f s r i k2 c4", k2=4, s=2, i=8, r=2)
        ident_full = ident[:, :].rearrange("p (a b c) -> p a b c", a=8, b=4)
        ident_chan = ident[:, :].rearrange("p (a b c) -> p a b c", a=16, b=2)
        lt_view = lt[:, :, :].rearrange("f g (r s w) -> f g r s w", r=2, s=2)
        ot_pool = ot_ps[:, :].rearrange("f (b s i r j) -> f s r b i j", b=2, s=2, i=8, r=2)
        ident_pool = ident[:, :].rearrange("p (a b c) -> p a b c", a=2, b=8)
        ident_pchan = ident[:, :].rearrange("p (a b c) -> p a b c", a=8, b=2)

        def plain(t, b, y):
            return t[:, b, :].rearrange("c (r y x z) -> c y r x z", y=2, x=PW, z=2)[:, y]

        def mixed(t, b, y):
            return t[:, b, :].rearrange("c (r x y z) -> c y r x z", x=PW, y=2, z=2)[:, y]

        def tokens(n, r, s):
            b, half = TILES[n]
            return lt_view[:, half, r, s] if b is None else xt_view[:, b, r, s, half]

        def query_key_operands(n, query, queries, i):
            to = qk[:, n % 2, :].rearrange("w (d q k h) -> w q k d h", d=HD, q=WIN, k=WIN)[:, query]
            q = queries[:, i * C:(i + 1) * C].rearrange("w (d h) -> w d h", d=HD).unsqueeze(1)
            keys = k_sb[:, n % 2, :].rearrange("w (k d h) -> w k d h", k=WIN, d=HD)
            return to, q.broadcast_to([P, WIN, HD, HEADS]), keys

        def halve(eng, engine, kind, n):
            if kind == "HS":
                products_done(eng, n)
                d = HD // 2 * NS
                low, high = qk[:, n % 2, 0:d], qk[:, n % 2, d:2 * d]
            elif kind == "HS2":
                sums_halved(eng, ("HS",), n)
                d = HD // 4 * NS
                low, high = qk[:, n % 2, 0:d], qk[:, n % 2, d:2 * d]
            else:
                if kind == "HV":
                    eng.wait_ge(pv_dve, n + 1)
                else:
                    sums_halved(eng, ("HV",), n)
                k = WIN // 2 if kind == "HV" else 1
                v = pv[:, n % 2, :].rearrange("w (q k f) -> w q k f", q=WIN, k=WIN)
                low, high = v[:, :, 0:k], v[:, :, k:2 * k]
            return engine.tensor_tensor(low, low, high, ALU.add)

        block = ctx.enter_context(nc.Block())

        @block.sync
        def _(sp):
            for i in range(2):
                sp.dma_start(x_sb[:, 0, i * 512:(i + 1) * 512], x_dram[0, :, i * 512:(i + 1) * 512]).then_inc(
                    x_loaded[0] if i == 0 else x0_rest, 16)
            for b in range(1, B):
                sp.dma_start(x_sb[:, b, :], x_dram[b]).then_inc(x_loaded[b], 16)
            sp.dma_start(bias_v[:, :], b_qkv[2 * C:3 * C].rearrange("(p a) -> p a", a=1)).then_inc(bv_loaded, 16)
            sp.dma_start(bias_p[:, :], b_proj.rearrange("(p a) -> p a", a=1)).then_inc(bp_loaded, 16)
            sp.dma_start(wp_sb[:, :], w_proj).then_inc(wp_loaded, 16)
            sp.dma_start(resize_sb[:, :, :], resize).then_inc(resize_loaded, 16)
            for b in range(B - 1):
                for half in range(2):
                    sp.wait_ge(job_dve, DVE_JOBS.index(("out", b, half)) + 1)
                sp.dma_start(out_dram[b], out_sb[:, b, :]).then_inc(out_stored, 16)
            for t, job in enumerate((("begin", LAST, 1), ("end", LAST, 1))):
                sp.wait_ge(job_dve, DVE_JOBS.index(job) + 1)
                sp.dma_start(out_dram[LAST, :, t * TOK:(t + 1) * TOK],
                             out_sb[:, LAST, t * TOK:(t + 1) * TOK]).then_inc(out_stored, 16)
            sp.wait_ge(out_stored, 16 * (B + 1))

        @block.gpsimd
        def _(pool):
            nc.gpsimd.memset(ident[:, :], 0.0).then_inc(consts_set, 1)
            nc.gpsimd.memset(group_mean[:, :], 1.0 / GROUP).then_inc(consts_set, 1)
            nc.gpsimd.memset(half_pow[:, :], -0.5).then_inc(consts_set, 1)
            nc.gpsimd.memset(ones3[:, :], 1.0).then_inc(consts_set, 1)
            pool.wait_ge(consts_set, 4)
            nc.gpsimd.affine_select(out=ident[:, :], in_=ident[:, :], compare_op=ALU.not_equal, fill=1.0, base=0,
                                    pattern=[[-1, P]], channel_multiplier=1).then_inc(consts_made, 1)
            gm = group_mean[:, :].rearrange("p (g c) -> p g c", c=GROUP)
            nc.gpsimd.affine_select(out=gm, in_=gm, compare_op=ALU.is_ge, fill=0.0, base=0,
                                    pattern=[[-GROUP, P // GROUP], [0, GROUP]],
                                    channel_multiplier=1).then_inc(consts_set, 1)
            pool.wait_ge(consts_set, 5)
            nc.gpsimd.affine_select(out=gm, in_=gm, compare_op=ALU.is_ge, fill=0.0, base=GROUP - 1,
                                    pattern=[[GROUP, P // GROUP], [0, GROUP]],
                                    channel_multiplier=-1).then_inc(consts_made, 1)
            pool.wait_ge(consts_made, 1)
            for a in range(2):
                at = slice(a * P // 2, (a + 1) * P // 2)
                nc.gpsimd.tensor_copy(mixer[:, at].rearrange("p (x y z) -> p x y z", x=PW, y=2),
                                      ident[:, at].rearrange("p (y x z) -> p x y z", y=2, x=PW)).then_inc(mixer_made, 1)

            def inverse_std(g):
                b0, nb = STATS[g]
                pool.wait_ge(job_dve, DVE_JOBS.index(("var", g)) + 1)
                if g == 2:
                    pool.wait_ge(neg_done, 1)
                nc.gpsimd.tensor_tensor(rstd[:, b0:b0 + nb], gvar[:, b0:b0 + nb], half_pow[:, b0:b0 + nb],
                                        ALU.pow).then_inc(rstd_done, 1)
                if g == 2:
                    pool.wait_ge(rstd_done, g + 1)
                    nc.gpsimd.tensor_tensor(offset[:, b0:b0 + nb], neg_mean[:, b0:b0 + nb], rstd[:, b0:b0 + nb],
                                            ALU.mult).then_inc(offset_done, 1)

            def query_key(n, i):
                pool.wait_ge(k_out, n + 1)
                pool.wait_ge(q_out, n + 1)
                if n >= 2:
                    pool.wait_ge(st_made, n - 1)
                nc.gpsimd.tensor_tensor(*query_key_operands(n, i, q_sb[:, n % 2, :], i - WIN + POOL_QUERIES),
                                        ALU.mult).then_inc(qk_pool, 1)

            for kind, *at in ORDER["POOL"]:
                if kind in halved_pool:
                    halve(pool, nc.gpsimd, kind, *at).then_inc(halved_pool[kind], 1)
                else:
                    {"std": inverse_std, "M": query_key}[kind](*at)

        @block.scalar
        def _(act):
            act.dma_start(bias_rows[:, :], b_qkv[0:2 * C].unsqueeze(0).broadcast_to([P, 2 * C])).then_inc(
                bias_loaded, 16)
            act.dma_start(w_sb[:, :], w_qkv).then_inc(w_loaded, 16)

            def weights(to, w):
                for a in range(2):
                    nc.scalar.copy(to[:, a, :].rearrange("c (d h) -> c d h", d=HD),
                                   w[:, a * C:(a + 1) * C].rearrange("c (h d) -> c d h", h=HEADS)).then_inc(wqk_made, 1)

            def weights_mixed():
                act.wait_ge(mix_made, 1)
                weights(wqk_mix, sm_ps[0])
                nc.scalar.copy(wv_mix[:, :], sm_ps[0][:, 2 * C:3 * C]).then_inc(wqk_made, 1)

            def weights_plain():
                act.wait_ge(w_loaded, 16)
                weights(wqk, w_sb)

            def read_job(job):
                act.wait_ge(job_made, JOBS.index(job) + 1)
                if job[0] == "xt":
                    _, b, side = job
                    nc.scalar.copy(xt_side[:, b, side], bank(job)[:, :].rearrange("f (r m) -> f r m", r=2)
                                   ).then_inc(job_act, 1)
                else:
                    nc.scalar.mul(lt[:, job[1], :], bank(job)[:, :], 0.25).then_inc(job_act, 1)

            def normalise(b, y):
                act.wait_ge(rstd_done, 3)
                act.wait_ge(offset_done, 1)
                nc.scalar.activation(mixed(xn, b, y), plain(x_sb, b, y), ACT.Identity, bias=offset[:, b:b + 1],
                                     scale=rstd[:, b:b + 1]).then_inc(xn_act, 1)

            def keys_out(n):
                act.wait_ge(k_made, n + 1)
                if n >= 2:
                    products_done(act, n - 2)
                nc.scalar.copy(k_sb[:, n % 2, :], k_ps[:, :]).then_inc(k_out, 1)

            def order_bias():
                act.wait_ge(bias_loaded, 16)
                nc.scalar.copy(bias_qk[:, :, :].rearrange("p a (d h) -> p a d h", d=HD),
                               bias_rows[:, :].rearrange("p (a h d) -> p a d h", a=2, h=HEADS)).then_inc(bias_made, 1)

            def seed(bank, a, done):
                act.wait_ge(bias_made, 1)
                act.wait_ge(bits_set, 1)
                nc.scalar.copy(bank[:, :].rearrange("w (q f) -> w q f", q=WIN),
                               bias_qk[:, a].unsqueeze(1).broadcast_to([P, WIN, C])).then_inc(done, 1)

            def seed_keys(n):
                if n >= 1:
                    act.wait_ge(k_out, n)
                seed(k_ps, 1, k_seeded)

            def seed_queries(n):
                if n >= 2:
                    act.wait_ge(q_out, n - 1)
                    act.wait_ge(qk_dve, n - 1)
                seed(q_ps[n % 2], 0, q_seeded)

            def queries_out(n):
                act.wait_ge(q_made, n + 1)
                if n >= 2:
                    products_done(act, n - 2)
                first = min([job[2] for job in ORDER["POOL"] if job[:2] == ("M", n)] + [WIN - 1])
                nc.scalar.copy(q_sb[:, n % 2, (first - WIN + POOL_QUERIES) * C:],
                               q_ps[n % 2][:, first * C:]).then_inc(q_out, 1)

            def values_out(n):
                act.wait_ge(v_made, n + 1)
                if n >= VBUF:
                    act.wait_ge(pv_dve, n - VBUF + 1)
                nc.scalar.copy(v_sb[:, n % VBUF, :], v_ps[:, :]).then_inc(v_out, 1)

            def scores_t_out(n):
                act.wait_ge(st_made, n + 1)
                if n >= 2:
                    act.wait_ge(s_made, n - 1)
                nc.scalar.copy(st_sb[:, n % 2, :], sm_ps[n % 2][:, ST]).then_inc(st_out, 1)

            def exponent(n):
                act.wait_ge(shift_done, n + 1)
                if n >= 2:
                    act.wait_ge(prob_done, n - 1)
                nc.scalar.activation(expd[:, n % 2, :], shifted[:, n % 2, :], ACT.Exp, scale=SCALE).then_inc(
                    exp_done, 1)

            def attention_out(n):
                act.wait_ge(ot_made, n + 1)
                act.wait_ge(bv_loaded, 16)
                nc.scalar.activation(ot[:, n, :], ot_ps[:, :], ACT.Identity, bias=bias_v[:, 0:1]).then_inc(ot_out, 1)

            for kind, *at in ORDER["ACT"]:
                if kind in ("xt", "lt"):
                    read_job((kind, *at))
                else:
                    {"wqk_mix": weights_mixed, "wqk": weights_plain, "norm": normalise, "K": keys_out,
                     "bias": order_bias, "SK": seed_keys, "SQ": seed_queries, "Q": queries_out,
                     "V": values_out, "S": scores_t_out, "X": exponent, "O": attention_out}[kind](*at)

        @block.vector
        def _(dve):
            def batch_stats(b0, nb=1):
                for b in range(b0, b0 + nb):
                    dve.wait_ge(x_loaded[b], 16)
                    for i in range(2):
                        if b == 0 and i == 1:
                            dve.wait_ge(x0_rest, 16)
                        nc.vector.bn_stats(bn[:, b, i, :], x_sb[:, b, i * 512:(i + 1) * 512]).then_inc(bn_done, 1)
                for b in range(b0, b0 + nb):
                    dve.wait_ge(bn_done, 2 * (b + 1))
                    nc.vector.bn_aggr(mv[:, b, :], bn[:, b, :, :].rearrange("p i s -> p (i s)")).then_inc(mv_done, 1)

            def spread(g):
                b0, nb = STATS[g]
                bs = slice(b0, b0 + nb)
                dve.wait_ge(job_made, JOBS.index(("mean", g)) + 1)
                dve.wait_ge(mv_done, b0 + nb)
                m = job_ps[:, 0:2 * nb].rearrange("p (b s) -> p b s", s=2)
                nc.vector.tensor_tensor(dev[:, bs], mv[:, bs, 0], m[:, :, 0], ALU.subtract).then_inc(dev_done, 1)
                if g == 2:
                    nc.vector.tensor_scalar(neg_mean[:, bs], m[:, :, 0], -1.0, None, ALU.mult).then_inc(neg_done, 1)
                nc.vector.tensor_copy(gstat[:, bs, :], m).then_inc(job_dve, 1)
                dve.wait_ge(dev_done, g + 1)
                nc.vector.tensor_tensor(dev2[:, bs], dev[:, bs], dev[:, bs], ALU.mult).then_inc(dev2_done, 1)

            def variance(g):
                b0, nb = STATS[g]
                bs = slice(b0, b0 + nb)
                dve.wait_ge(job_made, JOBS.index(("var", g)) + 1)
                dve.wait_ge(job_dve, DVE_JOBS.index(("mean", g)) + 1)
                nc.vector.scalar_tensor_tensor(out=gvar[:, bs], in0=job_ps[:, 0:nb], scalar=EPS, in1=gstat[:, bs, 1],
                                               op0=ALU.add, op1=ALU.add).then_inc(job_dve, 1)

            def normalise(b, y):
                dve.wait_ge(rstd_done, 1 + min(b, 2))
                nc.vector.tensor_scalar(mixed(xn, b, y), plain(x_sb, b, y), gstat[:, b, 0:1], rstd[:, b:b + 1],
                                        ALU.subtract, ALU.mult).then_inc(xn_dve, 1)

            def query_key(n, i):
                dve.wait_ge(q_out, n + 1)
                dve.wait_ge(k_out, n + 1)
                if n >= 2:
                    dve.wait_ge(st_made, n - 1)
                ins = nc.vector.tensor_tensor(*query_key_operands(n, i, q_ps[n % 2][:, :], i), ALU.mult)
                if ("M", n, i) == [item for item in ORDER["DVE"] if item[:2] == ("M", n)][-1]:
                    ins.then_inc(qk_dve, 1)

            def by_key(ap):
                return ap.rearrange("w (q k h) -> w q k h", q=WIN, k=WIN)

            def by_head(ap):
                return ap.rearrange("w (q h) -> w q h", q=WIN)

            def shift(n):
                dve.wait_ge(s_made, n + 1)
                sc = sm_ps[n % 2][:, SC]
                nc.vector.tensor_reduce(by_head(row_max[:, n % 2, :]),
                                        sc.rearrange("w (q k h) -> w q h k", q=WIN, k=WIN), AX.X,
                                        ALU.max).then_inc(max_done, 1)
                dve.wait_ge(max_done, n + 1)
                if n >= 2:
                    dve.wait_ge(exp_done, n - 1)
                nc.vector.tensor_tensor(by_key(shifted[:, n % 2, :]), by_key(sc),
                                        by_head(row_max[:, n % 2, :]).unsqueeze(2).broadcast_to([P, WIN, WIN, HEADS]),
                                        ALU.subtract).then_inc(shift_done, 1)

            def divide(n):
                dve.wait_ge(exp_done, n + 1)
                e = expd[:, n % 2, :]
                nc.vector.tensor_reduce(by_head(denom[:, n % 2, :]),
                                        e.rearrange("w (q k h) -> w q h k", q=WIN, k=WIN), AX.X,
                                        ALU.add).then_inc(denom_done, 1)
                dve.wait_ge(denom_done, n + 1)
                nc.vector.reciprocal(inv[:, n % 2, :], denom[:, n % 2, :]).then_inc(inv_done, 1)
                dve.wait_ge(inv_done, n + 1)
                nc.vector.tensor_tensor(by_key(sm_ps[n % 2][:, PR]), by_key(e),
                                        by_head(inv[:, n % 2, :]).unsqueeze(2).broadcast_to([P, WIN, WIN, HEADS]),
                                        ALU.mult).then_inc(prob_done, 1)

            def prob_value(n):
                dve.wait_ge(prob_done, n + 1)
                dve.wait_ge(v_out, n + 1)
                if n >= 2:
                    dve.wait_ge(ot_made, n - 1)
                shape = [P, WIN, WIN * HEADS, HD]
                p = sm_ps[n % 2][:, PR].rearrange("w (q kh) -> w q kh", q=WIN)
                v = v_sb[:, n % VBUF, :].rearrange("w (kh d) -> w kh d", d=HD)
                to, a, b = (pv[:, n % 2, :].rearrange("w (q kh d) -> w q kh d", q=WIN, d=HD),
                            p.unsqueeze(3).broadcast_to(shape), v.unsqueeze(1).broadcast_to(shape))
                if n < N - 1:
                    nc.vector.tensor_tensor(to, a, b, ALU.mult).then_inc(pv_dve, 1)
                else:
                    for q in range(WIN):
                        nc.vector.tensor_tensor(to[:, q], a[:, q], b[:, q], ALU.mult).then_inc(pv_last, 1)

            def result(job):
                kind, b, half = job
                cs = {"out": slice(0, C), "begin": slice(0, CH), "end": slice(CH, C)}[kind]
                ks = slice(half * K // 2, (half + 1) * K // 2)
                dve.wait_ge(job_made, JOBS.index(job) + 1)
                dve.wait_ge(bp_loaded, 16)
                nc.vector.scalar_tensor_tensor(
                    out=out_sb[:, b, :].rearrange("f (c k) -> f c k", k=K)[:, cs, ks],
                    in0=bank(job)[:, :].rearrange("f (k c) -> f c k", c=C)[:, cs], scalar=bias_p[:, 0:1],
                    in1=x_sb[:, b, :].rearrange("f (c k) -> f c k", k=K)[:, cs, ks],
                    op0=ALU.add, op1=ALU.add).then_inc(job_dve, 1)

            for kind, *at in ORDER["DVE"]:
                if kind in ("out", "begin", "end"):
                    result((kind, *at))
                elif kind in halved_dve:
                    halve(dve, nc.vector, kind, *at).then_inc(halved_dve[kind], 1)
                else:
                    {"bn": batch_stats, "mean": spread, "var": variance, "norm": normalise,
                     "M": query_key, "X": shift, "D": divide, "P": prob_value}[kind](*at)

        @block.tensor
        def _(pe):
            PE = ORDER["PE"]
            OUT_FIRST = among(PE, ("out", "low"))[0]

            def jobs_read(item, its_bank):
                jobs = [j for j in among(PE[:PE.index(item)], ("xt", "lt")) if bank(j) is its_bank]
                if jobs:
                    job_read(pe, jobs[-1])

            def job_begins(job):
                earlier = [j for j in JOBS[:JOBS.index(job)] if bank(j) is bank(job) and j[0] != "low"]
                if earlier:
                    job_read(pe, earlier[-1])

            def do_job(job):
                job_begins(job)
                values_before, values_summed = before(PE, job, ("V",)), before(PE, job, ("O",))
                if values_before and bank(job) is v_ps:
                    pe.wait_ge(v_out, values_before)
                if values_summed and bank(job) is ot_ps:
                    pe.wait_ge(ot_out, values_summed)
                if bank(job) is q_ps[0]:
                    products_done(pe, N - 2)
                    pe.wait_ge(q_out, N - 1)
                if bank(job) is k_ps:
                    pe.wait_ge(k_out, N)
                if job == OUT_FIRST:
                    pe.wait_ge(wp_loaded, 16)
                    pe.wait_ge(resize_loaded, 16)
                kind = job[0]
                if kind == "mean":
                    b0, nb = STATS[job[1]]
                    pe.wait_ge(mv_done, b0 + nb)
                    ins = nc.tensor.matmul(job_ps[:, 0:2 * nb], group_mean[:, :],
                                           mv[:, b0:b0 + nb, :].rearrange("p b s -> p (b s)"), start=True, stop=True)
                elif kind == "var":
                    b0, nb = STATS[job[1]]
                    pe.wait_ge(dev2_done, job[1] + 1)
                    ins = nc.tensor.matmul(job_ps[:, 0:nb], group_mean[:, :], dev2[:, b0:b0 + nb], start=True,
                                           stop=True)
                elif kind == "xt":
                    _, b, side = job
                    pe.wait_ge(*normalised(b))
                    to = bank(job)[:, :].rearrange("f (r n k2 c4) -> f k2 n r c4", r=2, n=16, k2=4)
                    for i in range(4):
                        k = 2 * i + side
                        ins = nc.tensor.matmul(to[:, i], xn[:, b, k * P:(k + 1) * P], ident_chan,
                                               is_transpose=True, start=True, stop=True, skip_group_check=True)
                elif kind == "lt":
                    g = job[1]
                    for b in (2 * g, 2 * g + 1):
                        pe.wait_ge(*normalised(b))
                    to = bank(job)[:, :].rearrange("f (r s b i j) -> f b s i r j", r=2, s=2, b=2, i=8)
                    for i in range(2):
                        rows = xn[:, 2 * g + i, :].rearrange("c (k m j) -> c k j m", k=KL, j=4)
                        for k in range(KL):
                            for j in range(4):
                                ins = nc.tensor.matmul(to[:, i, k], rows[:, k, j], ident_pchan, is_transpose=True,
                                                       start=(j == 0), stop=(j == 3), skip_group_check=True)
                else:
                    _, b, half = job
                    low = POOLED[b // 2]
                    tiles = [TILES.index((b, t)) for t in range(HALVES)]
                    if kind in ("out", "low"):
                        blocks = [i for i, (k, _) in enumerate(BLOCKS) if k // (K // 2) == half]
                        pe.wait_ge(ot_out, low + 1)
                        for i in blocks:
                            k, l = BLOCKS[i]
                            at = (k - half * K // 2) * C
                            low_ot = ot[:, low, :].rearrange("f (b l c) -> f b l c", b=2, l=KL)[:, b % 2, l]
                            ins = nc.tensor.matmul(bank(job)[:, at:at + C], resize_sb[:, i, :], low_ot,
                                                   start=(i == blocks[0]), stop=True, skip_group_check=True)
                    for t in {"low": (), "out": (0, 1), "begin": (0,), "end": (1,)}[kind]:
                        pe.wait_ge(ot_out, tiles[t] + 1)
                        ins = nc.tensor.matmul(
                            bank(job)[:, :].rearrange("f (k t c) -> f t k c", t=HALVES, c=CH)[:, t], wp_sb[:, :],
                            ot[:, tiles[t], :].rearrange("f (h k c) -> f h k c", h=2, c=CH)[:, half],
                            start=False, stop=True, skip_group_check=True)
                ins.then_inc(job_made, 1)

            def product(n, a, to):
                b, half = TILES[n]
                pe.wait_ge(wqk_made, 5 if b is None else 3)
                weights = wqk if b is None else wqk_mix
                for s in range(2):
                    job_read(pe, ("lt", half) if b is None else ("xt", b, s))
                    for r in range(2):
                        at = (2 * r + s) * C
                        ins = nc.tensor.matmul(to[:, at:at + C], tokens(n, r, s), weights[:, a, :], start=False,
                                               stop=True, skip_group_check=True)
                return ins

            def keys(n):
                pe.wait_ge(k_seeded, n + 1)
                product(n, 1, k_ps).then_inc(k_made, 1)

            def queries(n):
                pe.wait_ge(q_seeded, n + 1)
                product(n, 0, q_ps[n % 2]).then_inc(q_made, 1)

            def values(n):
                if n >= 1:
                    pe.wait_ge(v_out, n)
                jobs_read(("V", n), v_ps)
                for r in range(2):
                    for s in range(2):
                        at = (2 * r + s) * C
                        weights = w_sb[:, 2 * C:3 * C] if TILES[n][0] is None else wv_mix[:, :]
                        ins = nc.tensor.matmul(v_ps[:, at:at + C], tokens(n, r, s), weights,
                                               start=True, stop=True, skip_group_check=True)
                ins.then_inc(v_made, 1)

            def sum_scores(n):
                products_done(pe, n)
                terms = HD >> sums_halved(pe, ("HS", "HS2"), n)
                if n >= 2:
                    pe.wait_ge(pv_dve, n - 1)
                for d in range(terms):
                    ins = nc.tensor.matmul(sm_ps[n % 2][:, ST], qk[:, n % 2, d * NS:(d + 1) * NS], ident[:, :],
                                           is_transpose=True, start=(d == 0), stop=(d == terms - 1))
                ins.then_inc(st_made, 1)

            def turn_scores(n):
                pe.wait_ge(st_out, n + 1)
                nc.tensor.transpose(sm_ps[n % 2][:, SC], st_sb[:, n % 2, :], ident[:, :]).then_inc(s_made, 1)

            def sum_values(n):
                jobs_read(("O", n), ot_ps)
                if n < N - 1:
                    pe.wait_ge(pv_dve, n + 1)
                terms = WIN >> sums_halved(pe, ("HV", "HV2"), n)
                if n >= 1:
                    pe.wait_ge(ot_out, n)
                dst, eye = (ot_pool, ident_pool) if TILES[n][0] is None else (ot_full, ident_full)
                pv_n = pv[:, n % 2, :].rearrange("w (q k f) -> w q k f", q=WIN, k=WIN)
                for r in range(2):
                    for s in range(2):
                        if n == N - 1:
                            pe.wait_ge(pv_last, 2 * r + s + 1)
                        for k in range(terms):
                            ins = nc.tensor.matmul(dst[:, s, r], pv_n[:, 2 * r + s, k], eye, is_transpose=True,
                                                   start=(k == 0), stop=(k == terms - 1), skip_group_check=True)
                ins.then_inc(ot_made, 1)

            def keep_warm(n):
                for _ in range(n):
                    nc.tensor.matmul(sm_ps[1][:, ST], ident[:, :], ident[:, :], start=True, stop=True)

            def mix_weights():
                pe.wait_ge(mixer_made, 2)
                pe.wait_ge(w_loaded, 16)
                nc.tensor.matmul(sm_ps[0][:, 0:3 * C], mixer[:, :], w_sb[:, :], start=True, stop=True).then_inc(
                    mix_made, 1)

            pe.wait_ge(consts_set, 4)
            for to in (k_ps, *q_ps):
                ins = nc.tensor.matmul(to[:, :].rearrange("w (q f) -> w q f", q=WIN), ones3[:, :],
                                       ones3[:, :].unsqueeze(1).broadcast_to([3, WIN, C]), start=True, stop=True,
                                       skip_group_check=True)
            ins.then_inc(bits_set, 1)
            pe.wait_ge(consts_made, 1)
            for item in PE:
                keep_warm(WARM.get(item, 0))
                if item == ("mean", 0):
                    pe.wait_ge(consts_made, 2)
                kind, *at = item
                if item in JOBS:
                    do_job(item)
                else:
                    {"mix": mix_weights, "K": keys, "Q": queries, "V": values, "S": sum_scores, "T": turn_scores,
                     "O": sum_values}[kind](*at)


def kernel(**inputs):
    import concourse.bacc as bacc
    from concourse.bass_utils import run_bass_kernel_spmd

    nc = bacc.Bacc("TRN2", target_bir_lowering=False, num_devices=1)
    names = ["x", "L0_conv_Wqkv", "L0_conv_bqkv", "L0_conv_Wproj", "L0_conv_bproj"]
    arrays = {f"in_{name}": np.ascontiguousarray(inputs[name]) for name in names}
    arrays["in_resize"] = RESIZE
    args = [nc.dram_tensor(name, a.shape, F32, kind="ExternalInput").ap() for name, a in arrays.items()]
    args.append(nc.dram_tensor("out_0", (B, C, H, W), F32, kind="ExternalOutput").ap())
    conv_attention_kernel(nc, *args)
    r = run_bass_kernel_spmd(nc, [arrays], core_ids=[0])
    return r.results[0]["out_0"]
```
